# Optimizing a Trainium2 kernel written in Bass

```python
import numpy as np
import jax
import jax.numpy as jnp

def _softmax(x, axis=-1):
    return jax.nn.softmax(x, axis=axis)

def _gelu(x):
    return jax.nn.gelu(x, approximate=True)

def _silu(x):
    return jax.nn.silu(x)

def _sigmoid(x):
    return jax.nn.sigmoid(x)

def _layernorm(x, axis=-1, eps=1e-05):
    m = jnp.mean(x, axis=axis, keepdims=True)
    v = jnp.var(x, axis=axis, keepdims=True)
    return (x - m) / jnp.sqrt(v + eps)

def _scatter_add(tgt, idx, src, axis=0):
    return tgt.at[idx].add(src)

def _segment_sum(src, seg, n):
    return jax.ops.segment_sum(src, seg, n)
kernel_name = 'mk_sandwich_d1_jaxref_r8_e9f66d'

def setup_inputs(seed: int=0):
    np.random.seed(seed)
    _w = jnp.asarray

    def _L0_attn_setup():
        import jax, jax.numpy as jnp
        import numpy as np
        BLOCK = 32
        NUM_HEADS = 16
        HEAD_DIM = 128
        FP4_GRID = jnp.array([0.0, 0.5, 1.0, 1.5, 2.0, 3.0, 4.0, 6.0], dtype=jnp.float32)

        def quantize_to_mxfp4(w, block_size=BLOCK):
            D, F = w.shape
            blocks = w.reshape(D // block_size, block_size, F)
            amax = jnp.max(jnp.abs(blocks), axis=1)
            e = jnp.floor(jnp.log2(jnp.maximum(amax, 1e-12) / 6.0))
            scale = jnp.exp2(e)
            v = blocks / scale[:, None, :]
            idx = jnp.argmin(jnp.abs(jnp.abs(v)[..., None] - FP4_GRID), axis=-1)
            codes = jnp.sign(v) * FP4_GRID[idx]
            return (codes.reshape(D, F).astype(jnp.float32), scale.astype(jnp.float32))

        def _mxfp4_matmul(x, codes, scales, block_size=BLOCK):
            w = codes * jnp.repeat(scales, block_size, axis=0)
            return x @ w
        key = jax.random.key(seed)
        ks = jax.random.split(key, 9)
        B, S, D = (2, 256, 256)
        feat = NUM_HEADS * HEAD_DIM
        x = jax.random.normal(ks[0], (B, S, D), dtype=jnp.float32)

        def make_w(k, din, dout):
            w = jax.random.normal(k, (din, dout), dtype=jnp.float32) * (1.0 / np.sqrt(din))
            return quantize_to_mxfp4(w, BLOCK)
        wq_codes, wq_scales = make_w(ks[1], D, feat)
        wk_codes, wk_scales = make_w(ks[2], D, feat)
        wv_codes, wv_scales = make_w(ks[3], D, feat)
        wo_codes, wo_scales = make_w(ks[4], feat, D)
        bq = jnp.zeros((feat,), jnp.float32)
        bk = jnp.zeros((feat,), jnp.float32)
        bv = jnp.zeros((feat,), jnp.float32)
        bo = jnp.zeros((D,), jnp.float32)
        return {'x': x, 'wq_codes': wq_codes, 'wq_scales': wq_scales, 'bq': bq, 'wk_codes': wk_codes, 'wk_scales': wk_scales, 'bk': bk, 'wv_codes': wv_codes, 'wv_scales': wv_scales, 'bv': bv, 'wo_codes': wo_codes, 'wo_scales': wo_scales, 'bo': bo}
    _L0_attn_in = _L0_attn_setup()

    def _L0_ffn_setup():
        import jax, jax.numpy as jnp
        import numpy as np
        H = 256
        I = 176
        E = 8
        K = 2
        B, S = (2, 256)
        key = jax.random.key(seed)
        k0, k1, k2, k3, k4 = jax.random.split(key, 5)
        scale = 1.0 / np.sqrt(H)
        x = jax.random.normal(k0, (B, S, H), dtype=jnp.float32)
        Wr = jax.random.normal(k1, (H, E), dtype=jnp.float32) * scale
        Wg = jax.random.normal(k2, (E, H, I), dtype=jnp.float32) * scale
        Wu = jax.random.normal(k3, (E, H, I), dtype=jnp.float32) * scale
        Wd = jax.random.normal(k4, (E, I, H), dtype=jnp.float32) * (1.0 / np.sqrt(I))
        return {'x': x, 'Wr': Wr, 'Wg': Wg, 'Wu': Wu, 'Wd': Wd}
    _L0_ffn_in = _L0_ffn_setup()
    _d = {'L0_attn_x': _L0_attn_in['x'], 'L0_attn_wq_codes': _L0_attn_in['wq_codes'], 'L0_attn_wq_scales': _L0_attn_in['wq_scales'], 'L0_attn_bq': _L0_attn_in['bq'], 'L0_attn_wk_codes': _L0_attn_in['wk_codes'], 'L0_attn_wk_scales': _L0_attn_in['wk_scales'], 'L0_attn_bk': _L0_attn_in['bk'], 'L0_attn_wv_codes': _L0_attn_in['wv_codes'], 'L0_attn_wv_scales': _L0_attn_in['wv_scales'], 'L0_attn_bv': _L0_attn_in['bv'], 'L0_attn_wo_codes': _L0_attn_in['wo_codes'], 'L0_attn_wo_scales': _L0_attn_in['wo_scales'], 'L0_attn_bo': _L0_attn_in['bo'], 'L0_ffn_Wr': _L0_ffn_in['Wr'], 'L0_ffn_Wg': _L0_ffn_in['Wg'], 'L0_ffn_Wu': _L0_ffn_in['Wu'], 'L0_ffn_Wd': _L0_ffn_in['Wd']}
    _x0 = _d['L0_attn_x']
    _d['L0_attn_x'] = jax.random.normal(jax.random.fold_in(jax.random.key(seed), 1), (1, 2048, 256), dtype=_x0.dtype)
    del _x0
    return _d

def reference(L0_attn_x, L0_attn_wq_codes, L0_attn_wq_scales, L0_attn_bq, L0_attn_wk_codes, L0_attn_wk_scales, L0_attn_bk, L0_attn_wv_codes, L0_attn_wv_scales, L0_attn_bv, L0_attn_wo_codes, L0_attn_wo_scales, L0_attn_bo, L0_ffn_Wr, L0_ffn_Wg, L0_ffn_Wu, L0_ffn_Wd):

    def _L0_attn_ref(x, wq_codes, wq_scales, bq, wk_codes, wk_scales, bk, wv_codes, wv_scales, bv, wo_codes, wo_scales, bo):
        import jax, jax.numpy as jnp
        import numpy as np
        BLOCK = 32
        NUM_HEADS = 16
        HEAD_DIM = 128
        FP4_GRID = jnp.array([0.0, 0.5, 1.0, 1.5, 2.0, 3.0, 4.0, 6.0], dtype=jnp.float32)

        def quantize_to_mxfp4(w, block_size=BLOCK):
            D, F = w.shape
            blocks = w.reshape(D // block_size, block_size, F)
            amax = jnp.max(jnp.abs(blocks), axis=1)
            e = jnp.floor(jnp.log2(jnp.maximum(amax, 1e-12) / 6.0))
            scale = jnp.exp2(e)
            v = blocks / scale[:, None, :]
            idx = jnp.argmin(jnp.abs(jnp.abs(v)[..., None] - FP4_GRID), axis=-1)
            codes = jnp.sign(v) * FP4_GRID[idx]
            return (codes.reshape(D, F).astype(jnp.float32), scale.astype(jnp.float32))

        def _mxfp4_matmul(x, codes, scales, block_size=BLOCK):
            w = codes * jnp.repeat(scales, block_size, axis=0)
            return x @ w
        B, S, D = x.shape
        q = _mxfp4_matmul(x, wq_codes, wq_scales) + bq
        k = _mxfp4_matmul(x, wk_codes, wk_scales) + bk
        v = _mxfp4_matmul(x, wv_codes, wv_scales) + bv
        q = q.reshape(B, S, NUM_HEADS, HEAD_DIM)
        k = k.reshape(B, S, NUM_HEADS, HEAD_DIM)
        v = v.reshape(B, S, NUM_HEADS, HEAD_DIM)
        scores = jnp.einsum('bqhd,bkhd->bhqk', q, k) / jnp.sqrt(jnp.float32(HEAD_DIM))
        attn = jax.nn.softmax(scores, axis=-1)
        out = jnp.einsum('bhqk,bkhd->bqhd', attn, v).reshape(B, S, NUM_HEADS * HEAD_DIM)
        return _mxfp4_matmul(out, wo_codes, wo_scales) + bo

    def _L0_ffn_ref(x, Wr, Wg, Wu, Wd):
        import jax, jax.numpy as jnp
        import numpy as np
        H = 256
        I = 176
        E = 8
        K = 2
        B, S = (2, 256)
        router_logits = jnp.einsum('bsh,he->bse', x, Wr)
        probs = jax.nn.softmax(router_logits.astype(jnp.float32), axis=-1)
        topk_w, topk_idx = jax.lax.top_k(probs, K)
        topk_w = topk_w / jnp.sum(topk_w, axis=-1, keepdims=True)
        onehot = jax.nn.one_hot(topk_idx, E, dtype=topk_w.dtype)
        combine = jnp.einsum('bsk,bske->bse', topk_w, onehot)
        g = jnp.einsum('bsh,ehi->besi', x, Wg)
        u = jnp.einsum('bsh,ehi->besi', x, Wu)
        h = jax.nn.silu(g) * u
        y = jnp.einsum('besi,eih->besh', h, Wd)
        out = jnp.einsum('bse,besh->bsh', combine.astype(x.dtype), y)
        return out
    x = L0_attn_x
    x = x + _layernorm(_L0_attn_ref(_layernorm(x, axis=-1), L0_attn_wq_codes, L0_attn_wq_scales, L0_attn_bq, L0_attn_wk_codes, L0_attn_wk_scales, L0_attn_bk, L0_attn_wv_codes, L0_attn_wv_scales, L0_attn_bv, L0_attn_wo_codes, L0_attn_wo_scales, L0_attn_bo), axis=-1)
    x = x + _layernorm(_L0_ffn_ref(_layernorm(x, axis=-1), L0_ffn_Wr, L0_ffn_Wg, L0_ffn_Wu, L0_ffn_Wd), axis=-1)
    return x

_drawn_inputs = setup_inputs


def setup_inputs(seed=0):
    import zlib

    import numpy as np

    out = dict(_drawn_inputs(seed))
    spreads = {'L0_attn_bq': (0.0, 0.1),
     'L0_attn_bk': (0.0, 0.1),
     'L0_attn_bv': (0.0, 0.1),
     'L0_attn_bo': (0.0, 0.1)}
    factors = {}
    for name, (base, spread) in spreads.items():
        noise = np.random.default_rng([zlib.crc32(name.encode()), seed]).standard_normal(out[name].shape)
        drawn = base * np.exp(spread * noise) if base else spread * noise
        out[name] = jnp.asarray(drawn.astype(out[name].dtype))
    for name, factor in factors.items():
        out[name] = (out[name] * factor).astype(out[name].dtype)
    return out
```

```python
def sandwich_layer(nc, x, wq, sq, bq, wk, sk, bk, wv, sv, bv, wo, so, bo, wr, wg, wu, wd, out):
    from contextlib import ExitStack

    import concourse.bass as bass
    from concourse import mybir

    f32, f32r = mybir.dt.float32, mybir.dt.float32r
    ALU, ACT, AX = mybir.AluOpType, mybir.ActivationFunctionType, mybir.AxisListType

    P = 128
    S, D = x.shape[1], x.shape[2]
    FEAT = wq.shape[1]
    DH = 128
    H = FEAT // DH
    TT = S // P
    DC = D // P
    CH = 512
    NCH = S // CH
    TPC = CH // P
    KT = S // P
    HALF = S // 2
    Q8 = 2 * TPC
    BLOCK = D // sq.shape[0]
    NG = P // BLOCK
    E, I = wg.shape[0], wg.shape[2]
    IH = I // 2
    SCALE = float(DH) ** -0.5
    EPS = 1e-5
    RING = 4
    CHUNKS = H * NCH

    ctx = ExitStack()
    with ctx:
        ctx.enter_context(nc.allow_non_contiguous_dma(reason="per-head bias columns"))

        def sem(name):
            return ctx.enter_context(nc.semaphore(name))

        def sb(name, shape, dt, stack=ctx):
            return stack.enter_context(nc.sbuf_tensor(name, shape, dt))

        ident = sb("ident", [P, P], f32)
        zero = sb("zero", [P, 1], f32)
        xT_hi = sb("xT_hi", [P, DC, S], f32r)
        xT_lo = sb("xT_lo", [P, DC, S], f32r)
        acc = sb("acc", [P, TT, D], f32)
        stats = sb("stats", [P, TT, 6], f32)
        mv = sb("mv", [P, TT, 2], f32)
        std = sb("std", [P, TT], f32)
        rstd = sb("rstd", [P, TT], f32)
        att = ExitStack()
        probs = sb("probs", [P, 2, TPC, S], f32, att)
        kT_hi = sb("kT_hi", [P, S], f32r, att)
        kT_lo = sb("kT_lo", [P, S], f32r, att)
        v_hi = sb("v_hi", [P, KT, DH], f32r, att)
        v_lo = sb("v_lo", [P, KT, DH], f32r, att)
        v_full = sb("v_full", [P, TPC, DH], f32, att)
        qT_hi = sb("qT_hi", [P, CH], f32r, att)
        qT_lo = sb("qT_lo", [P, CH], f32r, att)
        pT_hi = sb("pT_hi", [P, RING, CH], f32r, att)
        pT_lo = sb("pT_lo", [P, RING, CH], f32r, att)
        oT_hi = sb("oT_hi", [P, CH], f32r, att)
        oT_lo = sb("oT_lo", [P, CH], f32r, att)
        bias_q = sb("bias_q", [P, H], f32, att)
        bias_k = sb("bias_k", [P, H], f32, att)
        bias_v = sb("bias_v", [P, FEAT], f32, att)
        part_max = sb("part_max", [P, 2, TPC, 2], f32, att)
        shift = sb("shift", [P, 2, TPC], f32, att)
        sums = sb("sums", [P, 2, TPC, 2], f32, att)
        total = sb("total", [P, 2, TPC], f32, att)
        rinv = sb("rinv", [P, 2, TPC], f32, att)
        KINDS = "kvqo"
        bias_now = {k: sb(f"bias_now_{k}", [P, 1], f32, att) for k in "kq"}
        codes = {k: sb(f"codes_{k}", [P, 2, P], f32, att) for k in KINDS}
        scales = {k: sb(f"scales_{k}", [P, 2, P], f32, att) for k in KINDS}
        w_hi = {k: sb(f"w_{k}_hi", [P, 2, P], f32r, att) for k in KINDS}
        w_lo = {k: sb(f"w_{k}_lo", [P, 2, P], f32r, att) for k in KINDS}
        x_in = probs[:, 1, 0:2, :].rearrange("p a (t d) -> p (a t) d", d=D)
        xn_in = probs[:, 1, 2:4, :].rearrange("p a (t d) -> p (a t) d", d=D)
        att.close()
        x_res = sb("x_res", [P, TT, D], f32)
        x1 = sb("x1", [P, TT, D], f32)
        xn2 = sb("xn2", [P, TT, D], f32)
        y = sb("y", [P, TT, D], f32)
        wr_raw = sb("wr_raw", [P, DC, E], f32)
        wr_hi = sb("wr_hi", [P, DC, E], f32r)
        wr_lo = sb("wr_lo", [P, DC, E], f32r)
        gu_raw = sb("gu_raw", [P, 2, DC, 2 * I], f32)
        gu_hi = sb("gu_hi", [P, 2, DC, 2 * I], f32r)
        gu_lo = sb("gu_lo", [P, 2, DC, 2 * I], f32r)
        d_raw = sb("d_raw", [IH, 2, 2, D], f32)
        d_hi = sb("d_hi", [IH, 2, 2, D], f32r)
        d_lo = sb("d_lo", [IH, 2, 2, D], f32r)
        lmax = sb("lmax", [P, TT], f32)
        ex = sb("ex", [P, TT, E], f32)
        cmp = sb("cmp", [P, E, TT, E], f32)
        comb = sb("comb", [P, TT, E], f32)
        wsum = sb("wsum", [P, TT], f32)
        gate = sb("gate", [P, 2, I], f32)
        hid = sb("hid", [P, 2, I], f32)
        hT_hi = sb("hT_hi", [IH, 2, 2, P], f32r)
        hT_lo = sb("hT_lo", [IH, 2, 2, P], f32r)

        ps_s = ctx.enter_context(nc.psum_tensor("ps_s", [P, S], f32))
        ps_t = ctx.enter_context(nc.psum_tensor("ps_t", [P, 2, CH], f32))
        ps_a = ctx.enter_context(nc.psum_tensor("ps_a", [P, 2, CH], f32))

        names = """x_loaded bo_loaded bias_loaded ident_set ident_ready stat_done aggr_done eps_done std_done rstd_done
            xn_done xn_t xT_hi_done xT_lo_done
            scores_ready max_part shift_ready p_ready t_ready pt_hi pt_lo pv_done out_hi out_lo
            total_done rinv_ready oproj_ready acc_done q_ready q_hi q_lo k_ready k_hi k_lo v_ready v_full_done
            v_lo_done
            res_loaded wr_loaded wr_hi_done wr_lo_done y_zero z_norm x1_done stat2 aggr2 eps2 std2 rstd2 aggr1 stat1 eps1
            std1 rstd1 xn2_done xn2_t xT2_hi xT2_lo logits_ready lmax_done lsub_done ex_done rank_step sel_done
            comb_step comb_ready gu_split_hi gu_split_lo gu_ready gu_gate h_gate h_ready h_t hT_hi_done hT_lo_done
            down_ready y_done stat3 aggr3 eps3 std3 rstd3 yn_done out_ready out_stored""".split()
        sm = {n: sem(n) for n in names}
        w_loaded = {k: sem(f"w_{k}_loaded") for k in KINDS}
        w_scaled = {k: sem(f"w_{k}_scaled") for k in KINDS}
        w_hi_done = {k: sem(f"w_{k}_hi_done") for k in KINDS}
        w_ready = {k: sem(f"w_{k}_ready") for k in KINDS}
        gu_loaded = [sem(f"gu_loaded{u}") for u in range(2)]

        block = ctx.enter_context(nc.Block())

        def full(ap):
            return ap.bitcast(f32)

        def wait(eng, name, value):
            if not isinstance(value, int) or value > 0:
                eng.wait_ge(sm[name] if isinstance(name, str) else name, value)

        def heads(eng, body):
            body(-1)
            body(0)
            with eng.Fori(1, H - 1) as h:
                body(h)
            body(H - 1)
            body(H)

        def experts(eng, body):
            body(0)
            with eng.Fori(1, E // 2) as i:
                body(i)

        def chunks_of(h):
            return [NCH - 1] if isinstance(h, int) and h < 0 else [0] if isinstance(h, int) and h == H else range(NCH)

        def has(h, j, ahead=0):
            return not isinstance(h, int) or 0 <= h * NCH + j + ahead < CHUNKS

        @block.sync
        def _(sp):
            xv = x[0].rearrange("(t p) d -> p t d", p=P)
            sp.dma_start(x_in, xv).then_inc(sm["x_loaded"], 16)
            src = {"k": (wk, sk), "v": (wv, sv), "q": (wq, sq)}

            def load(k, h):
                if k == "o":
                    sp.dma_start(codes[k][:, :, :].rearrange("p c n -> p (c n)"),
                                 wo[bass.ds(h * P, P), :]).then_inc(w_loaded[k], 16)
                    for g in range(NG):
                        sp.dma_start(scales[k][g * BLOCK:(g + 1) * BLOCK, :, :].rearrange("p c n -> p (c n)"),
                                     so[bass.ds(h * NG + g, 1), :].to_broadcast([BLOCK, D]))\
                            .then_inc(w_loaded[k], 16)
                else:
                    w, s = src[k]
                    sp.dma_start(codes[k][:, :, :],
                                 w.rearrange("(c p) f -> p c f", p=P)[:, :, bass.ds(h * DH, DH)])\
                        .then_inc(w_loaded[k], 16)
                    for g in range(NG):
                        row = s.rearrange("(c g) f -> g c f", g=NG)[g:g + 1, :, bass.ds(h * DH, DH)]
                        sp.dma_start(scales[k][g * BLOCK:(g + 1) * BLOCK, :, :],
                                     row.to_broadcast([BLOCK, DC, DH])).then_inc(w_loaded[k], 16)

            load("k", 0)
            load("q", 0)
            load("v", 0)
            for dst, b in ((bias_q, bq), (bias_k, bk)):
                sp.dma_start(dst[:, :], b.rearrange("(h p) -> p h", p=P)).then_inc(sm["bias_loaded"], 16)
            sp.dma_start(bias_v[:, :], bv.rearrange("(a n) -> a n", a=1).to_broadcast([P, FEAT]))\
                .then_inc(sm["bias_loaded"], 16)
            load("o", 0)
            sp.dma_start(acc[:, :, :], bo.rearrange("(a b n) -> a b n", a=1, b=1).to_broadcast([P, TT, D]))\
                .then_inc(sm["bo_loaded"], 16)
            with sp.Fori(1, H) as h:
                for k in "kvqo":
                    wait(sp, w_ready[k], h)
                    load(k, h)

            sp.wait_ge(sm["acc_done"], 2 * CHUNKS)
            sp.wait_ge(sm["out_hi"], CHUNKS)
            sp.wait_ge(w_ready["o"], H)
            sp.dma_start(x_res[:, :, :], xv).then_inc(sm["res_loaded"], 16)
            sp.dma_start(wr_raw[:, :, :], wr.rearrange("(c p) e -> p c e", p=P)).then_inc(sm["wr_loaded"], 16)

            def load_expert(e, u):
                for n, w in enumerate((wg, wu)):
                    sp.dma_start(gu_raw[:, u, :, n * I:(n + 1) * I],
                                 w[bass.ds(e, 1), :, :].rearrange("a (c p) i -> p (a c) i", p=P))\
                        .then_inc(gu_loaded[u], 16)
                sp.dma_start(d_raw[:, u, :, :],
                             wd[bass.ds(e, 1), :, :].rearrange("a (c p) n -> p (a c) n", p=IH))\
                    .then_inc(gu_loaded[u], 16)

            load_expert(0, 0)
            load_expert(1, 1)
            with sp.Fori(1, E // 2) as i:
                for u in range(2):
                    wait(sp, "gu_ready", 2 * i + u - 1)
                    load_expert(2 * i + u, u)
            ov = out[0].rearrange("(t p) d -> p t d", p=P)
            for t in range(0, TT, 4):
                sp.wait_ge(sm["out_ready"], t + 4)
                sp.dma_start(ov[:, t:t + 4, :], xn2[:, t:t + 4, :]).then_inc(sm["out_stored"], 16)
            sp.wait_ge(sm["out_stored"], 16 * (TT // 4))

        @block.gpsimd
        def _(pool):
            pool.memset(zero[:, :], 0.0).then_inc(sm["ident_set"], 1)
            pool.memset(ident[:, :], 0.0).then_inc(sm["ident_set"], 1)
            pool.wait_ge(sm["ident_set"], 2)
            pool.affine_select(out=ident[:, :], in_=ident[:, :], compare_op=ALU.not_equal, fill=1.0,
                               base=0, pattern=[[-1, P]], channel_multiplier=1).then_inc(sm["ident_ready"], 1)

            def weights(k, h):
                wait(pool, w_loaded[k], 16 * (NG + 1) * (h + 1))
                if not isinstance(h, int) or h > 0:
                    wait(pool, {"k": "k_lo", "v": "v_ready", "q": "q_lo", "o": "oproj_ready"}[k],
                         2 * NCH * h if k == "o" else NCH * h)
                pool.tensor_tensor(w_hi[k][:, :, :], codes[k][:, :, :], scales[k][:, :, :], ALU.mult)\
                    .then_inc(w_hi_done[k], 1)
                if k in bias_now:
                    src = {"q": bias_q, "k": bias_k}[k]
                    pool.tensor_copy(bias_now[k][:, :], src[:, bass.ds(h, 1)])
                wait(pool, w_hi_done[k], h + 1)
                pool.tensor_tensor(codes[k][:, :, :], codes[k][:, :, :], scales[k][:, :, :], ALU.mult)\
                    .then_inc(w_scaled[k], 1)
                wait(pool, w_scaled[k], h + 1)
                pool.tensor_tensor(w_lo[k][:, :, :], codes[k][:, :, :], full(w_hi[k][:, :, :]), ALU.subtract)\
                    .then_inc(w_ready[k], 1)

            def values(h, g):
                n = TPC * h + g
                wait(pool, "v_full_done", n + 1)
                pool.tensor_tensor(v_lo[:, g * TPC:(g + 1) * TPC, :], v_full[:, :, :],
                                   full(v_hi[:, g * TPC:(g + 1) * TPC, :]), ALU.subtract)\
                    .then_inc(sm["v_lo_done"], 1)

            pool.wait_ge(sm["bias_loaded"], 48)
            for k in KINDS:
                weights(k, 0)

            def body(h):
                first, end = isinstance(h, int) and h <= 0, isinstance(h, int) and h == H
                if end:
                    return
                if not (isinstance(h, int) and h < 0):
                    values(h, TPC - 1)
                    if not first:
                        weights("o", h)
                    if not (isinstance(h, int) and h == H - 1):
                        for k in "kvq":
                            weights(k, h + 1)
                if not (isinstance(h, int) and h == H - 1):
                    for g in range(TPC - 1):
                        values(h + 1, g)

            heads(pool, body)

            pool.wait_ge(sm["acc_done"], 2 * CHUNKS)
            pool.wait_ge(sm["out_hi"], CHUNKS)
            pool.memset(y[:, :, :], 0.0).then_inc(sm["y_zero"], 1)
            pool.wait_ge(sm["wr_loaded"], 16)
            pool.tensor_copy(wr_hi[:, :, :], wr_raw[:, :, :]).then_inc(sm["wr_hi_done"], 1)
            pool.wait_ge(sm["wr_hi_done"], 1)
            pool.tensor_tensor(wr_lo[:, :, :], wr_raw[:, :, :], full(wr_hi[:, :, :]), ALU.subtract)\
                .then_inc(sm["wr_lo_done"], 1)

            def residual(t):
                pool.wait_ge(sm["z_norm"], t + 1)
                pool.tensor_tensor(x1[:, t, :], x_res[:, t, :], acc[:, t, :], ALU.add).then_inc(sm["x1_done"], 1)

            def split_expert(i, u):
                e = 2 * i + u
                wait(pool, gu_loaded[u], 48 * (i + 1))
                if not (isinstance(i, int) and i == 0):
                    wait(pool, "down_ready", TT * (e - 1))
                pool.tensor_tensor(gu_hi[:, u, :, :], gu_raw[:, u, :, :], zero[:, :].unsqueeze(1).to_broadcast([P, DC, 2 * I]),
                                   ALU.add).then_inc(sm["gu_split_hi"], 1)
                pool.tensor_tensor(d_hi[:, u, :, :], d_raw[:, u, :, :], zero[0:IH, :].unsqueeze(1).to_broadcast([IH, 2, D]),
                                   ALU.add).then_inc(sm["gu_split_hi"], 1)
                wait(pool, "gu_split_hi", 2 * e + 2)
                pool.tensor_tensor(gu_lo[:, u, :, :], gu_raw[:, u, :, :], full(gu_hi[:, u, :, :]), ALU.subtract)\
                    .then_inc(sm["gu_split_lo"], 1)
                pool.tensor_tensor(d_lo[:, u, :, :], d_raw[:, u, :, :], full(d_hi[:, u, :, :]), ALU.subtract)\
                    .then_inc(sm["gu_ready"], 1)

            pool.wait_ge(sm["res_loaded"], 16)
            for t in range(TT):
                residual(t)
            def pair(i):
                split_expert(i, 0)
                split_expert(i, 1)

            experts(pool, pair)

        @block.tensor
        def _(pe):
            def product3(dst, lhs_hi, lhs_lo, rhs_hi, rhs_lo, first=True, last=True):
                nc.tensor.matmul(dst, lhs_hi, rhs_hi, start=first, stop=False)
                nc.tensor.matmul(dst, lhs_hi, rhs_lo, start=False, stop=False)
                return nc.tensor.matmul(dst, lhs_lo, rhs_hi, start=False, stop=last)

            def turn_tiles(done, src, group, sem_in, sem_out, evacuated):
                for c in range(DC):
                    n = DC * group + c
                    wait(pe, sem_in, TPC * group + TPC)
                    wait(pe, evacuated, n - 1)
                    for a in range(TPC):
                        last = nc.tensor.transpose(ps_t[:, n % 2, a * P:(a + 1) * P],
                                                   src[:, TPC * group + a, c * P:(c + 1) * P], ident[:, :])
                    last.then_inc(sm[sem_out], 1)

            pe.wait_ge(sm["ident_ready"], 1)
            for group in range(NCH):
                turn_tiles(None, xn_in, group, "xn_done", "xn_t", "xT_lo_done")
            pe.wait_ge(sm["xT_lo_done"], DC * NCH)

            def proj(dst, k, cols):
                for c in range(DC):
                    last = product3(dst, w_hi[k][:, c, :], w_lo[k][:, c, :], xT_hi[:, c, cols], xT_lo[:, c, cols],
                                    first=c == 0, last=c == DC - 1)
                return last

            def q_proj(h, j):
                m = NCH * h + j
                wait(pe, w_ready["q"], h + 1)
                free_side(h, j)
                proj(ps_a[:, (j + 1) % 2, :], "q", slice(j * CH, (j + 1) * CH)).then_inc(sm["q_ready"], 1)

            def free_side(h, j):
                m = NCH * h + j - 2
                wait(pe, "out_lo", m)
                wait(pe, "acc_done", 2 * m)
                if j in (0, 1):
                    wait(pe, "v_full_done", TPC * h + TPC - 1 if j == 1 else TPC * h)

            def k_proj(h):
                wait(pe, w_ready["k"], h + 1)
                for b in range(NCH):
                    wait(pe, "p_ready", Q8 * NCH * h - 2 + b // 2 + 1)
                    proj(ps_s[:, b * CH:(b + 1) * CH], "k", slice(b * CH, (b + 1) * CH)).then_inc(sm["k_ready"], 1)

            def v_proj(h, g, bank):
                wait(pe, w_ready["v"], h + 1)
                for a in range(TPC):
                    rows = slice((g * TPC + a) * P, (g * TPC + a + 1) * P)
                    for c in range(DC):
                        last = product3(ps_a[:, bank, a * DH:(a + 1) * DH], xT_hi[:, c, rows], xT_lo[:, c, rows],
                                        w_hi["v"][:, c, :], w_lo["v"][:, c, :], first=c == 0, last=c == DC - 1)
                last.then_inc(sm["v_ready"], 1)

            def scores(h, j, r, u):
                m = NCH * h + j
                if r == 0 and u == 0:
                    wait(pe, "q_lo", m + 1)
                if j == 0 and r == 0:
                    wait(pe, "k_lo", NCH * h + 2 * (u + 1))
                wait(pe, "p_ready", Q8 * m + 2 * r + u - 1)
                for b in range(2 * u, 2 * u + 2):
                    cols = slice(b * CH, (b + 1) * CH)
                    last = product3(ps_s[:, cols], qT_hi[:, r * P:(r + 1) * P], qT_lo[:, r * P:(r + 1) * P],
                                    kT_hi[:, cols], kT_lo[:, cols])
                last.then_inc(sm["scores_ready"], 1)

            def turn_probs(h, j, k):
                n = KT * (NCH * h + j) + k
                if k == 0:
                    wait(pe, "p_ready", Q8 * (NCH * h + j + 1))
                wait(pe, "pt_lo", n - 1)
                for a in range(TPC):
                    last = nc.tensor.transpose(ps_t[:, k % 2, a * P:(a + 1) * P],
                                               probs[:, j % 2, a, k * P:(k + 1) * P], ident[:, :])
                last.then_inc(sm["t_ready"], 1)

            def weighted_values(h, j, k):
                n = KT * (NCH * h + j) + k
                if k == 0:
                    m = NCH * h + j
                    if has(h, j, 1):
                        wait(pe, "q_lo", m + 2)
                    wait(pe, "acc_done", 2 * (m - 1))
                    if j == 0:
                        wait(pe, "v_full_done", TPC * h + TPC - 1)
                    if j == 1:
                        wait(pe, "v_full_done", TPC * h + TPC)
                if j == 0 and k % TPC == 0:
                    wait(pe, "v_lo_done", TPC * h + k // TPC + 1)
                wait(pe, "pt_lo", n + 1)
                product3(ps_a[:, j % 2, :], v_hi[:, k, :], v_lo[:, k, :], pT_hi[:, k % RING, :], pT_lo[:, k % RING, :],
                         first=k == 0, last=k == KT - 1).then_inc(sm["pv_done"], 1)

            def out_proj(h, j, i):
                m = NCH * h + j - 1
                hp = h if j else h - 1
                wait(pe, "out_lo", m + 1)
                wait(pe, w_ready["o"], hp + 1)
                wait(pe, "acc_done", 2 * m + i)
                if i == 1 and j == NCH - 1 and has(h, j, 1):
                    wait(pe, "v_full_done", TPC * (h + 1) + 1)
                if i == 0 and j == 0 and has(h, j):
                    wait(pe, "v_full_done", TPC * h + TPC)
                for a in range(2):
                    rows = slice((2 * i + a) * P, (2 * i + a + 1) * P)
                    last = product3(ps_a[:, (j + 1) % 2, a * D:(a + 1) * D], oT_hi[:, rows], oT_lo[:, rows],
                                    w_hi["o"][:, :, :].rearrange("p c n -> p (c n)"),
                                    w_lo["o"][:, :, :].rearrange("p c n -> p (c n)"))
                last.then_inc(sm["oproj_ready"], 1)

            def body(h):
                for j in chunks_of(h):
                    nxt = (h, j + 1) if j < NCH - 1 else (h + 1, 0)
                    after = (h, j + 2) if j < NCH - 2 else (h + 1, j + 2 - NCH)
                    if isinstance(h, int) and h < 0:
                        q_proj(0, 0)
                    for q in range(Q8):
                        def keys():
                            for k in (2 * q, 2 * q + 1):
                                if k >= 2 and has(h, j):
                                    weighted_values(h, j, k - 2)
                                if k < 2 and has(h, j, -1):
                                    weighted_values(*((h, j - 1) if j else (h - 1, NCH - 1)), KT - 2 + k)
                                if has(h, j):
                                    turn_probs(h, j, k)
                        new_head = j == NCH - 1 and q == 0 and has(h, j, 1)
                        if new_head:
                            keys()
                            k_proj(h + 1)
                        if has(h, j, 1):
                            scores(*nxt, q // 2, q % 2)
                        if q == Q8 - 1 and has(h, j, 2):
                            q_proj(*after)
                        if not new_head:
                            keys()
                        if q in (2, 4) and has(h, j, -1):
                            out_proj(h, j, q // 2 - 1)
                        if j == NCH - 1 and q in (3, 5, 6) and has(h, j, 1):
                            g = {3: 0, 5: 1, 6: 2}[q]
                            if has(h, j, -1):
                                wait(pe, "acc_done", 2 * (NCH * h + j - 1) + (1 if g == 0 else 2))
                            if g:
                                wait(pe, "v_full_done", TPC * (h + 1) + g)
                            elif not has(h, j):
                                wait(pe, "q_lo", 1)
                            v_proj(h + 1, g, (j + 1) % 2)
                        if j == 0 and q == 1 and has(h, j):
                            wait(pe, "out_lo", NCH * h)
                            if isinstance(h, int) and h == 0:
                                wait(pe, "q_lo", 2)
                            v_proj(h, TPC - 1, (j + 1) % 2)

            heads(pe, body)

            for group in range(NCH):
                turn_tiles(None, xn2, group, "xn2_done", "xn2_t", "xT2_lo")
            pe.wait_ge(sm["xT2_lo"], DC * NCH)
            pe.wait_ge(sm["wr_lo_done"], 1)
            for t in range(TT):
                rows = slice(t * P, (t + 1) * P)
                for c in range(DC):
                    last = product3(ps_s[:, t * E:(t + 1) * E], xT_hi[:, c, rows], xT_lo[:, c, rows],
                                    wr_hi[:, c, :], wr_lo[:, c, :], first=c == 0, last=c == DC - 1)
            last.then_inc(sm["logits_ready"], 1)
            pe.wait_ge(sm["lsub_done"], 1)

            def gate_up(e, u, t):
                n = TT * e + t
                if t == 0:
                    wait(pe, "gu_ready", e + 1)
                wait(pe, "h_ready", n - 2)
                rows = slice(t * P, (t + 1) * P)
                b = t % 2
                for c in range(DC):
                    last = product3(ps_s[:, b * CH:b * CH + 2 * I], xT_hi[:, c, rows], xT_lo[:, c, rows],
                                    gu_hi[:, u, c, :], gu_lo[:, u, c, :], first=c == 0, last=c == DC - 1)
                last.then_inc(sm["h_gate"], 1)

            def turn_hidden(e, u, t):
                n = TT * e + t
                wait(pe, "h_ready", n + 1)
                wait(pe, "hT_lo_done", n - 1)
                for c in range(2):
                    last = nc.tensor.transpose(ps_t[0:IH, t % 2, c * P:(c + 1) * P],
                                               hid[:, t % 2, c * IH:(c + 1) * IH], ident[:, :])
                last.then_inc(sm["h_t"], 1)

            def down(e, u, t):
                n = TT * e + t
                wait(pe, "hT_lo_done", n + 1)
                wait(pe, "y_done", n - 1)
                for c in range(2):
                    last = product3(ps_a[:, t % 2, 0:D], hT_hi[:, t % 2, c, :], hT_lo[:, t % 2, c, :],
                                    d_hi[:, u, c, :], d_lo[:, u, c, :], first=c == 0, last=c == 1)
                last.then_inc(sm["down_ready"], 1)

            def pair(i):
                for u in range(2):
                    e = 2 * i + u
                    for t in range(TT + 2):
                        if t < TT:
                            gate_up(e, u, t)
                        if 1 <= t <= TT:
                            turn_hidden(e, u, t - 1)
                        if t >= 2:
                            down(e, u, t - 2)

            experts(pe, pair)

        @block.scalar
        def _(act):
            act.wait_ge(sm["eps_done"], 1)
            nc.scalar.activation(std[:, :], std[:, :], ACT.Sqrt).then_inc(sm["std_done"], 1)

            def turned(n, sem_in, sem_out):
                act.wait_ge(sm[sem_in], n + 1)
                group, c = n // DC, n % DC
                nc.scalar.activation(xT_hi[:, c, group * CH:(group + 1) * CH], ps_t[:, n % 2, :], ACT.Copy)\
                    .then_inc(sm[sem_out], 1)

            for n in range(DC * NCH):
                turned(n, "xn_t", "xT_hi_done")

            def exps(h, j, r):
                m = NCH * h + j
                wait(act, "shift_ready", TPC * m + r + 1)
                if r == 0:
                    wait(act, "t_ready", KT * (m - 1))
                for u in range(2):
                    nc.scalar.activation(probs[:, j % 2, r, u * HALF:(u + 1) * HALF], ps_s[:, u * HALF:(u + 1) * HALF],
                                         ACT.Exp, bias=shift[:, j % 2, r:r + 1], scale=SCALE,
                                         accum_out=sums[:, j % 2, r, u:u + 1]).then_inc(sm["p_ready"], 1)

            def probs_hi(h, j, k):
                n = KT * (NCH * h + j) + k
                wait(act, "t_ready", n + 1)
                wait(act, "pv_done", n - RING + 1)
                nc.scalar.activation(pT_hi[:, k % RING, :], ps_t[:, k % 2, :], ACT.Copy).then_inc(sm["pt_hi"], 1)

            def out_hi(h, j):
                m = NCH * h + j - 1
                wait(act, "pv_done", KT * (m + 1))
                wait(act, "oproj_ready", 2 * m)
                nc.scalar.activation(oT_hi[:, :], ps_a[:, (j + 1) % 2, :], ACT.Copy).then_inc(sm["out_hi"], 1)

            def q_hi(h, j):
                wait(act, "q_ready", NCH * h + j + 1)
                nc.scalar.activation(qT_hi[:, :], ps_a[:, (j + 1) % 2, :], ACT.Identity,
                                     bias=bias_now["q"][:, :]).then_inc(sm["q_hi"], 1)

            def k_hi(h, b):
                wait(act, "k_ready", NCH * h + b + 1)
                cols = slice(b * CH, (b + 1) * CH)
                nc.scalar.activation(kT_hi[:, cols], ps_s[:, cols], ACT.Identity,
                                     bias=bias_now["k"][:, :]).then_inc(sm["k_hi"], 1)

            def body(h):
                for j in chunks_of(h):
                    nxt = (h, j + 1) if j < NCH - 1 else (h + 1, 0)
                    after = (h, j + 2) if j < NCH - 2 else (h + 1, j + 2 - NCH)
                    if isinstance(h, int) and h < 0:
                        q_hi(0, 0)
                    for q in range(Q8):
                        if q == 0 and has(h, j):
                            exps(h, j, TPC - 1)
                        if q % 2 == 0 and q and has(h, j, 1):
                            exps(*nxt, q // 2 - 1)
                        if q == 0 and has(h, j, -1):
                            out_hi(h, j)
                        if q == Q8 - 1 and has(h, j, 2):
                            q_hi(*after)
                        if has(h, j):
                            probs_hi(h, j, 2 * q)
                            probs_hi(h, j, 2 * q + 1)
                        if j == NCH - 1 and q == 0 and has(h, j, 1):
                            for b in range(NCH):
                                k_hi(h + 1, b)

            heads(act, body)

            for s_in, s_out in (("eps1", "std1"), ("eps2", "std2")):
                act.wait_ge(sm[s_in], 1)
                nc.scalar.activation(std[:, :], std[:, :], ACT.Sqrt).then_inc(sm[s_out], 1)
            for n in range(DC * NCH):
                turned(n, "xn2_t", "xT2_hi")
            act.wait_ge(sm["lsub_done"], 1)
            nc.scalar.activation(ex[:, :, :], ex[:, :, :], ACT.Exp).then_inc(sm["ex_done"], 1)

            def gates(e, t):
                n = TT * e + t
                wait(act, "h_gate", n + 1)
                wait(act, "h_ready", n - 1)
                nc.scalar.activation(gate[:, t % 2, :], ps_s[:, (t % 2) * CH:(t % 2) * CH + I], ACT.Silu)\
                    .then_inc(sm["gu_gate"], 1)

            def hidden_hi(e, t):
                n = TT * e + t
                wait(act, "h_t", n + 1)
                wait(act, "down_ready", n - 1)
                nc.scalar.activation(hT_hi[:, t % 2, :, :],
                                     ps_t[0:IH, t % 2, 0:2 * P].rearrange("p (c n) -> p c n", c=2), ACT.Copy)\
                    .then_inc(sm["hT_hi_done"], 1)

            def pair(i):
                for u in range(2):
                    e = 2 * i + u
                    for t in range(TT + 1):
                        if t < TT:
                            gates(e, t)
                        if t >= 1:
                            hidden_hi(e, t - 1)
            experts(act, pair)
            act.wait_ge(sm["eps3"], 1)
            nc.scalar.activation(std[:, :], std[:, :], ACT.Sqrt).then_inc(sm["std3"], 1)

        @block.vector
        def _(dve):
            V = nc.vector

            def moments(src, t, s_stat, s_aggr, ready=None):
                if ready is not None:
                    dve.wait_ge(sm[ready[0]], ready[1])
                V.bn_stats(stats[:, t, :], src[:, t, :]).then_inc(sm[s_stat], 1)
                dve.wait_ge(sm[s_stat], t + 1)
                V.bn_aggr(mv[:, t, :], stats[:, t, :]).then_inc(sm[s_aggr], 1)

            def inverse_std(s_aggr, s_eps, s_std, s_rstd):
                dve.wait_ge(sm[s_aggr], TT)
                V.tensor_scalar(std[:, :], mv[:, :, 1], EPS, None, ALU.add).then_inc(sm[s_eps], 1)
                dve.wait_ge(sm[s_std], 1)
                V.reciprocal(rstd[:, :], std[:, :]).then_inc(sm[s_rstd], 1)
                dve.wait_ge(sm[s_rstd], 1)

            def normed(dst, src, t):
                return V.tensor_scalar(dst[:, t, :], src[:, t, :], mv[:, t, 0:1], rstd[:, t:t + 1],
                                       ALU.subtract, ALU.mult)

            def turned_lo(n, sem_in, sem_out):
                dve.wait_ge(sm[sem_in], n + 1)
                group, c = n // DC, n % DC
                cols = slice(group * CH, (group + 1) * CH)
                V.tensor_tensor(xT_lo[:, c, cols], ps_t[:, n % 2, :], full(xT_hi[:, c, cols]), ALU.subtract)\
                    .then_inc(sm[sem_out], 1)

            dve.wait_ge(sm["x_loaded"], 16)
            for t in range(TT):
                moments(x_in, t, "stat_done", "aggr_done")
            inverse_std("aggr_done", "eps_done", "std_done", "rstd_done")
            for t in range(TT):
                normed(xn_in, x_in, t).then_inc(sm["xn_done"], 1)
            for n in range(DC * NCH):
                turned_lo(n, "xT_hi_done", "xT_lo_done")
            dve.wait_ge(sm["bo_loaded"], 16)
            dve.wait_ge(sm["bias_loaded"], 48)

            def half_max(h, j, r, u):
                n = Q8 * (NCH * h + j) + 2 * r + u
                wait(dve, "scores_ready", n + 1)
                V.tensor_reduce(part_max[:, j % 2, r, u:u + 1], ps_s[:, u * HALF:(u + 1) * HALF], AX.X, ALU.max)\
                    .then_inc(sm["max_part"], 1)

            def row_shift(h, j, r):
                wait(dve, "max_part", Q8 * (NCH * h + j) + 2 * r + 2)
                V.tensor_scalar(shift[:, j % 2, r:r + 1], part_max[:, j % 2, r, 0:1], part_max[:, j % 2, r, 1:2],
                                -SCALE, ALU.max, ALU.mult).then_inc(sm["shift_ready"], 1)

            def probs_lo(h, j, k):
                n = KT * (NCH * h + j) + k
                wait(dve, "pt_hi", n + 1)
                V.tensor_tensor(pT_lo[:, k % RING, :], ps_t[:, k % 2, :], full(pT_hi[:, k % RING, :]), ALU.subtract)\
                    .then_inc(sm["pt_lo"], 1)

            def out_lo(h, j):
                wait(dve, "out_hi", NCH * h + j)
                V.tensor_tensor(oT_lo[:, :], ps_a[:, (j + 1) % 2, :], full(oT_hi[:, :]), ALU.subtract)\
                    .then_inc(sm["out_lo"], 1)

            def row_sums(h, j):
                m = NCH * h + j
                wait(dve, "p_ready", Q8 * (m + 1))
                V.tensor_tensor(total[:, j % 2, :], sums[:, j % 2, :, 0], sums[:, j % 2, :, 1], ALU.add)\
                    .then_inc(sm["total_done"], 1)
                wait(dve, "total_done", m + 1)
                V.reciprocal(rinv[:, j % 2, :], total[:, j % 2, :]).then_inc(sm["rinv_ready"], 1)

            def add_out(h, j, i):
                m = NCH * h + j - 1
                jp = (j - 1) % NCH
                wait(dve, "oproj_ready", 2 * m + i + 1)
                if i == 0:
                    wait(dve, "rinv_ready", m + 1)
                for a in range(2):
                    t = jp * TPC + 2 * i + a
                    ins = V.scalar_tensor_tensor(acc[:, t, :], ps_a[:, (j + 1) % 2, a * D:(a + 1) * D],
                                                 rinv[:, jp % 2, 2 * i + a:2 * i + a + 1], acc[:, t, :],
                                                 ALU.mult, ALU.add)
                ins.then_inc(sm["acc_done"], 1)

            def q_lo(h, j):
                wait(dve, "q_hi", NCH * h + j + 1)
                V.scalar_tensor_tensor(qT_lo[:, :], ps_a[:, (j + 1) % 2, :], bias_now["q"][:, :], full(qT_hi[:, :]),
                                       ALU.add, ALU.subtract).then_inc(sm["q_lo"], 1)

            def k_lo(h, b):
                wait(dve, "k_hi", NCH * h + b + 1)
                cols = slice(b * CH, (b + 1) * CH)
                V.scalar_tensor_tensor(kT_lo[:, cols], ps_s[:, cols], bias_now["k"][:, :], full(kT_hi[:, cols]),
                                       ALU.add, ALU.subtract).then_inc(sm["k_lo"], 1)

            def values(h, g, bank):
                n = TPC * h + g
                wait(dve, "v_ready", n + 1)
                wait(dve, "v_lo_done", n)
                src = ps_a[:, bank, :].rearrange("p (a d) -> p a d", d=DH)
                bias = bias_v[:, bass.ds(h * DH, DH)].unsqueeze(1).to_broadcast([P, TPC, DH])
                V.tensor_tensor(v_hi[:, g * TPC:(g + 1) * TPC, :], src, bias, ALU.add)
                V.tensor_tensor(v_full[:, :, :], src, bias, ALU.add).then_inc(sm["v_full_done"], 1)

            def body(h):
                for j in chunks_of(h):
                    nxt = (h, j + 1) if j < NCH - 1 else (h + 1, 0)
                    after = (h, j + 2) if j < NCH - 2 else (h + 1, j + 2 - NCH)
                    if isinstance(h, int) and h < 0:
                        q_lo(0, 0)
                    for q in range(Q8):
                        new_head = j == NCH - 1 and q == 0 and has(h, j, 1)
                        if not new_head and has(h, j, 1):
                            half_max(*nxt, q // 2, q % 2)
                            if q % 2:
                                row_shift(*nxt, q // 2)
                        if q == 0 and has(h, j, -1):
                            out_lo(h, j)
                        if q in (3, 5) and has(h, j, -1):
                            add_out(h, j, (q - 3) // 2)
                        if j == NCH - 1 and has(h, j, 1) and q in (4, 6, 7):
                            values(h + 1, {4: 0, 6: 1, 7: 2}[q], (j + 1) % 2)
                        if j == 0 and q == 2 and has(h, j):
                            values(h, TPC - 1, (j + 1) % 2)
                        if q == Q8 - 1 and has(h, j, 2):
                            q_lo(*after)
                        if has(h, j):
                            probs_lo(h, j, 2 * q)
                            probs_lo(h, j, 2 * q + 1)
                            if q == 1:
                                row_sums(h, j)
                        if new_head:
                            for b in range(NCH):
                                k_lo(h + 1, b)
                            half_max(*nxt, 0, 0)

            heads(dve, body)

            dve.wait_ge(sm["acc_done"], 2 * CHUNKS)
            for t in range(TT):
                moments(acc, t, "stat1", "aggr1")
            inverse_std("aggr1", "eps1", "std1", "rstd1")
            for t in range(TT):
                normed(acc, acc, t).then_inc(sm["z_norm"], 1)
            for t in range(TT):
                moments(x1, t, "stat2", "aggr2", ("x1_done", t + 1))
            inverse_std("aggr2", "eps2", "std2", "rstd2")
            for t in range(TT):
                normed(xn2, x1, t).then_inc(sm["xn2_done"], 1)
            for n in range(DC * NCH):
                turned_lo(n, "xT2_hi", "xT2_lo")

            dve.wait_ge(sm["logits_ready"], 1)
            logits = ps_s[:, 0:TT * E].rearrange("p (t e) -> p t e", e=E)
            V.tensor_reduce(lmax[:, :], logits, AX.X, ALU.max).then_inc(sm["lmax_done"], 1)
            dve.wait_ge(sm["lmax_done"], 1)
            V.tensor_tensor(ex[:, :, :], logits, lmax[:, :].unsqueeze(2).to_broadcast([P, TT, E]), ALU.subtract)\
                .then_inc(sm["lsub_done"], 1)
            dve.wait_ge(sm["ex_done"], 1)
            steps = 0
            for a in range(E):
                for lo, hi, op in ((0, a + 1, ALU.is_gt), (a + 1, E, ALU.is_ge)):
                    if lo < hi:
                        V.tensor_tensor(cmp[:, a, :, lo:hi], ex[:, :, a:a + 1].to_broadcast([P, TT, hi - lo]),
                                        ex[:, :, lo:hi], op).then_inc(sm["rank_step"], 1)
                        steps += 1
            half = E // 2
            while half:
                dve.wait_ge(sm["rank_step"], steps)
                V.tensor_tensor(cmp[:, 0:half, :, :], cmp[:, 0:half, :, :], cmp[:, half:2 * half, :, :], ALU.add)\
                    .then_inc(sm["rank_step"], 1)
                steps += 1
                half //= 2
            dve.wait_ge(sm["rank_step"], steps)
            V.scalar_tensor_tensor(comb[:, :, :], cmp[:, 0, :, :], 1.5, ex[:, :, :], ALU.is_lt, ALU.mult)\
                .then_inc(sm["sel_done"], 1)
            dve.wait_ge(sm["sel_done"], 1)
            V.tensor_reduce(wsum[:, :], comb[:, :, :], AX.X, ALU.add).then_inc(sm["comb_step"], 1)
            dve.wait_ge(sm["comb_step"], 1)
            V.reciprocal(wsum[:, :], wsum[:, :]).then_inc(sm["comb_step"], 1)
            dve.wait_ge(sm["comb_step"], 2)
            V.tensor_tensor(comb[:, :, :], comb[:, :, :], wsum[:, :].unsqueeze(2).to_broadcast([P, TT, E]), ALU.mult)\
                .then_inc(sm["comb_ready"], 1)
            dve.wait_ge(sm["comb_ready"], 1)
            dve.wait_ge(sm["y_zero"], 1)

            def hidden(e, t):
                n = TT * e + t
                wait(dve, "gu_gate", n + 1)
                wait(dve, "h_t", n - 1)
                V.scalar_tensor_tensor(hid[:, t % 2, :], gate[:, t % 2, :], comb[:, t, bass.ds(e, 1)],
                                       ps_s[:, (t % 2) * CH + I:(t % 2) * CH + 2 * I], ALU.mult, ALU.mult)\
                    .then_inc(sm["h_ready"], 1)

            def hidden_lo(e, t):
                n = TT * e + t
                wait(dve, "hT_hi_done", n + 1)
                V.tensor_tensor(hT_lo[:, t % 2, :, :], ps_t[0:IH, t % 2, 0:2 * P].rearrange("p (c n) -> p c n", c=2),
                                full(hT_hi[:, t % 2, :, :]), ALU.subtract).then_inc(sm["hT_lo_done"], 1)

            def add_expert(e, t):
                wait(dve, "down_ready", TT * e + t + 1)
                V.tensor_tensor(y[:, t, :], ps_a[:, t % 2, 0:D], y[:, t, :], ALU.add).then_inc(sm["y_done"], 1)

            def pair(i):
                for u in range(2):
                    e = 2 * i + u
                    for t in range(TT + 2):
                        if t < TT:
                            hidden(e, t)
                        if 1 <= t <= TT:
                            hidden_lo(e, t - 1)
                        if t >= 2:
                            add_expert(e, t - 2)

            experts(dve, pair)

            dve.wait_ge(sm["y_done"], TT * E)
            for t in range(TT):
                moments(y, t, "stat3", "aggr3")
            inverse_std("aggr3", "eps3", "std3", "rstd3")
            for t in range(TT):
                normed(y, y, t).then_inc(sm["yn_done"], 1)
                dve.wait_ge(sm["yn_done"], t + 1)
                V.tensor_tensor(xn2[:, t, :], x1[:, t, :], y[:, t, :], ALU.add).then_inc(sm["out_ready"], 1)


_INS = ["x", "wq_codes", "wq_scales", "bq", "wk_codes", "wk_scales", "bk", "wv_codes", "wv_scales", "bv",
        "wo_codes", "wo_scales", "bo"]
_FFN = ["Wr", "Wg", "Wu", "Wd"]


def kernel(**inputs):
    import numpy as np
    import concourse.bacc as bacc
    from concourse import mybir
    from concourse.bass_utils import run_bass_kernel_spmd

    nc = bacc.Bacc("TRN2", target_bir_lowering=False, num_devices=1)
    arrays, aps = {}, []
    for name in [f"L0_attn_{n}" for n in _INS] + [f"L0_ffn_{n}" for n in _FFN]:
        a = np.ascontiguousarray(inputs[name])
        arrays[f"in_{name}"] = a
        aps.append(nc.dram_tensor(f"in_{name}", a.shape, mybir.dt.from_np(a.dtype), kind="ExternalInput").ap())
    shape = inputs["L0_attn_x"].shape
    aps.append(nc.dram_tensor("layer_out", shape, mybir.dt.float32, kind="ExternalOutput").ap())
    sandwich_layer(nc, *aps)
    r = run_bass_kernel_spmd(nc, [arrays], core_ids=[0])
    return r.results[0]["layer_out"]
```

```python
def sandwich_layer(nc, x, wq, sq, bq, wk, sk, bk, wv, sv, bv, wo, so, bo, wr, wg, wu, wd, out):
    from contextlib import ExitStack

    import concourse.bass as bass
    from concourse import mybir

    f32, f32r = mybir.dt.float32, mybir.dt.float32r
    ALU, ACT, AX = mybir.AluOpType, mybir.ActivationFunctionType, mybir.AxisListType

    P = 128
    S, D = x.shape[1], x.shape[2]
    FEAT = wq.shape[1]
    DH = 128
    H = FEAT // DH
    TT = S // P
    DC = D // P
    CH = 512
    NCH = S // CH
    TPC = CH // P
    KT = S // P
    HALF = S // 2
    MAX_PARTS = [(0, HALF), (HALF, HALF + CH), (HALF + CH, S)]
    EXP_PARTS = [(0, CH), (CH, HALF), (HALF, S)]
    NP = len(MAX_PARTS)
    PART_OF_BANK = [0, 1, 2, 2]
    BLOCK = D // sq.shape[0]
    NG = P // BLOCK
    E, I = wg.shape[0], wg.shape[2]
    IH = I // 2
    SCALE = float(DH) ** -0.5
    EPS = 1e-5
    RING = 4
    CHUNKS = H * NCH

    ctx = ExitStack()
    with ctx:
        ctx.enter_context(nc.allow_non_contiguous_dma(reason="per-head bias columns"))

        def sem(name):
            return ctx.enter_context(nc.semaphore(name))

        def sb(name, shape, dt, stack=ctx):
            return stack.enter_context(nc.sbuf_tensor(name, shape, dt))

        ident = sb("ident", [P, P], f32)
        zero = sb("zero", [P, 1], f32)
        xT_hi = sb("xT_hi", [P, DC, S], f32r)
        xT_lo = sb("xT_lo", [P, DC, S], f32r)
        acc = sb("acc", [P, TT, D], f32)
        stats = sb("stats", [P, TT, 6], f32)
        mv = sb("mv", [P, TT, 2], f32)
        std = sb("std", [P, TT], f32)
        rstd = sb("rstd", [P, TT], f32)
        att = ExitStack()
        probs = sb("probs", [P, 2, TPC, S], f32, att)
        kT_hi = sb("kT_hi", [P, S], f32r, att)
        kT_lo = sb("kT_lo", [P, S], f32r, att)
        v_hi = sb("v_hi", [P, KT, DH], f32r, att)
        v_lo = sb("v_lo", [P, KT, DH], f32r, att)
        v_full = sb("v_full", [P, TPC, DH], f32, att)
        qT_hi = sb("qT_hi", [P, CH], f32r, att)
        qT_lo = sb("qT_lo", [P, CH], f32r, att)
        pT_hi = sb("pT_hi", [P, RING, CH], f32r, att)
        pT_lo = sb("pT_lo", [P, RING, CH], f32r, att)
        oT_hi = sb("oT_hi", [P, CH], f32r, att)
        oT_lo = sb("oT_lo", [P, CH], f32r, att)
        bias_q = sb("bias_q", [P, H], f32, att)
        bias_k = sb("bias_k", [P, H], f32, att)
        bias_v = sb("bias_v", [P, FEAT], f32, att)
        part_max = sb("part_max", [P, 2, TPC, NP + 1], f32, att)
        shift = sb("shift", [P, 2, TPC], f32, att)
        sums = sb("sums", [P, 2, TPC, NP], f32, att)
        total = sb("total", [P, 2, TPC], f32, att)
        rinv = sb("rinv", [P, 2, TPC], f32, att)
        KINDS = "kvqo"
        bias_now = {k: sb(f"bias_now_{k}", [P, 1], f32, att) for k in "kq"}
        codes = {k: sb(f"codes_{k}", [P, 2, P], f32, att) for k in KINDS}
        scales = {k: sb(f"scales_{k}", [P, 2, P], f32, att) for k in KINDS}
        w_hi = {k: sb(f"w_{k}_hi", [P, 2, P], f32r, att) for k in KINDS}
        w_lo = {k: sb(f"w_{k}_lo", [P, 2, P], f32r, att) for k in KINDS}
        x_in = probs[:, 1, 0:2, :].rearrange("p a (t d) -> p (a t) d", d=D)
        xn_in = probs[:, 1, 2:4, :].rearrange("p a (t d) -> p (a t) d", d=D)
        att.close()
        x_res = sb("x_res", [P, TT, D], f32)
        x1 = sb("x1", [P, TT, D], f32)
        xn2 = sb("xn2", [P, TT, D], f32)
        y = sb("y", [P, TT, D], f32)
        wr_raw = sb("wr_raw", [P, DC, E], f32)
        wr_hi = sb("wr_hi", [P, DC, E], f32r)
        wr_lo = sb("wr_lo", [P, DC, E], f32r)
        gu_raw = sb("gu_raw", [P, 2, DC, 2 * I], f32)
        gu_hi = sb("gu_hi", [P, 2, DC, 2 * I], f32r)
        gu_lo = sb("gu_lo", [P, 2, DC, 2 * I], f32r)
        d_raw = sb("d_raw", [IH, 2, 2, D], f32)
        d_hi = sb("d_hi", [IH, 2, 2, D], f32r)
        d_lo = sb("d_lo", [IH, 2, 2, D], f32r)
        lmax = sb("lmax", [P, TT], f32)
        ex = sb("ex", [P, TT, E], f32)
        cmp = sb("cmp", [P, E, TT, E], f32)
        comb = sb("comb", [P, TT, E], f32)
        wsum = sb("wsum", [P, TT], f32)
        gate = sb("gate", [P, 2, I], f32)
        hid = sb("hid", [P, 2, I], f32)
        hT_hi = sb("hT_hi", [IH, 2, 2, P], f32r)
        hT_lo = sb("hT_lo", [IH, 2, 2, P], f32r)

        ps_s = ctx.enter_context(nc.psum_tensor("ps_s", [P, S], f32))
        ps_t = ctx.enter_context(nc.psum_tensor("ps_t", [P, 2, CH], f32))
        ps_a = ctx.enter_context(nc.psum_tensor("ps_a", [P, 2, CH], f32))

        names = """bo_loaded bias_loaded ident_set ident_ready stat_done aggr_done eps_done std_done rstd_done
            xn_done xn_t xT_hi_done xT_lo_done
            scores_ready max_part max_first shift_ready p_ready t_ready pt_hi pt_lo pv_done out_hi out_lo
            total_done rinv_ready oproj_ready acc_done q_ready q_hi q_lo k_ready k_hi k_lo v_ready v_full_done
            v_lo_done
            res_loaded wr_loaded wr_hi_done wr_lo_done y_zero z_norm x1_done stat2 aggr2 eps2 std2 rstd2 aggr1 stat1 eps1
            std1 rstd1 xn2_done xn2_t xT2_hi xT2_lo logits_ready lmax_done lsub_done ex_done rank_step sel_done
            comb_step comb_ready gu_split_hi gu_split_lo gu_ready gu_gate h_gate h_ready h_t hT_hi_done hT_lo_done
            down_ready y_done stat3 aggr3 eps3 std3 rstd3 yn_done out_ready out_stored""".split()
        sm = {n: sem(n) for n in names}
        w_loaded = {k: sem(f"w_{k}_loaded") for k in KINDS}
        w_scaled = {k: sem(f"w_{k}_scaled") for k in KINDS}
        w_hi_done = {k: sem(f"w_{k}_hi_done") for k in KINDS}
        w_ready = {k: sem(f"w_{k}_ready") for k in KINDS}
        x_loaded = [sem(f"x_loaded{g}") for g in range(NCH)]
        gu_loaded = [sem(f"gu_loaded{u}") for u in range(2)]

        block = ctx.enter_context(nc.Block())

        def full(ap):
            return ap.bitcast(f32)

        def wait(eng, name, value):
            if not isinstance(value, int) or value > 0:
                eng.wait_ge(sm[name] if isinstance(name, str) else name, value)

        def heads(eng, body):
            body(-1)
            body(0)
            with eng.Fori(1, H - 1) as h:
                body(h)
            body(H - 1)
            body(H)

        def experts(eng, body):
            body(0)
            with eng.Fori(1, E // 2) as i:
                body(i)

        def chunks_of(h):
            return [NCH - 1] if isinstance(h, int) and h < 0 else [0] if isinstance(h, int) and h == H else range(NCH)

        def has(h, j, ahead=0):
            return not isinstance(h, int) or 0 <= h * NCH + j + ahead < CHUNKS

        @block.sync
        def _(sp):
            xv = x[0].rearrange("(t p) d -> p t d", p=P)
            for g in range(NCH):
                rows = slice(g * TPC, (g + 1) * TPC)
                sp.dma_start(x_in[:, rows, :], xv[:, rows, :]).then_inc(x_loaded[g], 16)
            src = {"k": (wk, sk), "v": (wv, sv), "q": (wq, sq)}

            def load(k, h):
                if k == "o":
                    sp.dma_start(codes[k][:, :, :].rearrange("p c n -> p (c n)"),
                                 wo[bass.ds(h * P, P), :]).then_inc(w_loaded[k], 16)
                    for g in range(NG):
                        sp.dma_start(scales[k][g * BLOCK:(g + 1) * BLOCK, :, :].rearrange("p c n -> p (c n)"),
                                     so[bass.ds(h * NG + g, 1), :].to_broadcast([BLOCK, D]))\
                            .then_inc(w_loaded[k], 16)
                else:
                    w, s = src[k]
                    sp.dma_start(codes[k][:, :, :],
                                 w.rearrange("(c p) f -> p c f", p=P)[:, :, bass.ds(h * DH, DH)])\
                        .then_inc(w_loaded[k], 16)
                    for g in range(NG):
                        row = s.rearrange("(c g) f -> g c f", g=NG)[g:g + 1, :, bass.ds(h * DH, DH)]
                        sp.dma_start(scales[k][g * BLOCK:(g + 1) * BLOCK, :, :],
                                     row.to_broadcast([BLOCK, DC, DH])).then_inc(w_loaded[k], 16)

            load("k", 0)
            load("q", 0)
            load("v", 0)
            for dst, b in ((bias_q, bq), (bias_k, bk)):
                sp.dma_start(dst[:, :], b.rearrange("(h p) -> p h", p=P)).then_inc(sm["bias_loaded"], 16)
            sp.dma_start(bias_v[:, :], bv.rearrange("(a n) -> a n", a=1).to_broadcast([P, FEAT]))\
                .then_inc(sm["bias_loaded"], 16)
            load("o", 0)
            sp.dma_start(acc[:, :, :], bo.rearrange("(a b n) -> a b n", a=1, b=1).to_broadcast([P, TT, D]))\
                .then_inc(sm["bo_loaded"], 16)
            with sp.Fori(1, H) as h:
                for k in "kvqo":
                    wait(sp, w_ready[k], h)
                    load(k, h)

            sp.wait_ge(sm["acc_done"], 2 * CHUNKS)
            sp.wait_ge(sm["out_hi"], CHUNKS)
            sp.wait_ge(w_ready["o"], H)
            sp.dma_start(x_res[:, :, :], xv).then_inc(sm["res_loaded"], 16)
            sp.dma_start(wr_raw[:, :, :], wr.rearrange("(c p) e -> p c e", p=P)).then_inc(sm["wr_loaded"], 16)

            def load_expert(e, u):
                for n, w in enumerate((wg, wu)):
                    sp.dma_start(gu_raw[:, u, :, n * I:(n + 1) * I],
                                 w[bass.ds(e, 1), :, :].rearrange("a (c p) i -> p (a c) i", p=P))\
                        .then_inc(gu_loaded[u], 16)
                sp.dma_start(d_raw[:, u, :, :],
                             wd[bass.ds(e, 1), :, :].rearrange("a (c p) n -> p (a c) n", p=IH))\
                    .then_inc(gu_loaded[u], 16)

            load_expert(0, 0)
            load_expert(1, 1)
            with sp.Fori(1, E // 2) as i:
                for u in range(2):
                    wait(sp, "gu_ready", 2 * i + u - 1)
                    load_expert(2 * i + u, u)
            ov = out[0].rearrange("(t p) d -> p t d", p=P)
            for t in range(0, TT, 4):
                sp.wait_ge(sm["out_ready"], t + 4)
                sp.dma_start(ov[:, t:t + 4, :], xn2[:, t:t + 4, :]).then_inc(sm["out_stored"], 16)
            sp.wait_ge(sm["out_stored"], 16 * (TT // 4))

        @block.gpsimd
        def _(pool):
            pool.memset(zero[:, :], 0.0).then_inc(sm["ident_set"], 1)
            pool.memset(ident[:, :], 0.0).then_inc(sm["ident_set"], 1)
            pool.wait_ge(sm["ident_set"], 2)
            pool.affine_select(out=ident[:, :], in_=ident[:, :], compare_op=ALU.not_equal, fill=1.0,
                               base=0, pattern=[[-1, P]], channel_multiplier=1).then_inc(sm["ident_ready"], 1)

            def weights(k, h):
                wait(pool, w_loaded[k], 16 * (NG + 1) * (h + 1))
                if not isinstance(h, int) or h > 0:
                    wait(pool, {"k": "k_lo", "v": "v_ready", "q": "q_lo", "o": "oproj_ready"}[k],
                         2 * NCH * h if k == "o" else NCH * h)
                pool.tensor_tensor(w_hi[k][:, :, :], codes[k][:, :, :], scales[k][:, :, :], ALU.mult)\
                    .then_inc(w_hi_done[k], 1)
                if k in bias_now:
                    src = {"q": bias_q, "k": bias_k}[k]
                    pool.tensor_copy(bias_now[k][:, :], src[:, bass.ds(h, 1)])
                wait(pool, w_hi_done[k], h + 1)
                pool.tensor_tensor(codes[k][:, :, :], codes[k][:, :, :], scales[k][:, :, :], ALU.mult)\
                    .then_inc(w_scaled[k], 1)
                wait(pool, w_scaled[k], h + 1)
                pool.tensor_tensor(w_lo[k][:, :, :], codes[k][:, :, :], full(w_hi[k][:, :, :]), ALU.subtract)\
                    .then_inc(w_ready[k], 1)

            def values(h, g):
                n = TPC * h + g
                wait(pool, "v_full_done", n + 1)
                pool.tensor_tensor(v_lo[:, g * TPC:(g + 1) * TPC, :], v_full[:, :, :],
                                   full(v_hi[:, g * TPC:(g + 1) * TPC, :]), ALU.subtract)\
                    .then_inc(sm["v_lo_done"], 1)

            pool.wait_ge(sm["bias_loaded"], 48)
            for k in KINDS:
                weights(k, 0)

            def body(h):
                first, end = isinstance(h, int) and h <= 0, isinstance(h, int) and h == H
                if end:
                    return
                if not (isinstance(h, int) and h < 0):
                    values(h, TPC - 1)
                    if not first:
                        weights("o", h)
                    if not (isinstance(h, int) and h == H - 1):
                        for k in "kvq":
                            weights(k, h + 1)
                if not (isinstance(h, int) and h == H - 1):
                    for g in range(TPC - 1):
                        values(h + 1, g)

            heads(pool, body)

            pool.wait_ge(sm["acc_done"], 2 * CHUNKS)
            pool.wait_ge(sm["out_hi"], CHUNKS)
            pool.memset(y[:, :, :], 0.0).then_inc(sm["y_zero"], 1)
            pool.wait_ge(sm["wr_loaded"], 16)
            pool.tensor_copy(wr_hi[:, :, :], wr_raw[:, :, :]).then_inc(sm["wr_hi_done"], 1)
            pool.wait_ge(sm["wr_hi_done"], 1)
            pool.tensor_tensor(wr_lo[:, :, :], wr_raw[:, :, :], full(wr_hi[:, :, :]), ALU.subtract)\
                .then_inc(sm["wr_lo_done"], 1)

            def residual(t):
                pool.wait_ge(sm["z_norm"], t + 1)
                pool.tensor_tensor(x1[:, t, :], x_res[:, t, :], acc[:, t, :], ALU.add).then_inc(sm["x1_done"], 1)

            def split_expert(i, u):
                e = 2 * i + u
                wait(pool, gu_loaded[u], 48 * (i + 1))
                if not (isinstance(i, int) and i == 0):
                    wait(pool, "down_ready", TT * (e - 1))
                pool.tensor_tensor(gu_hi[:, u, :, :], gu_raw[:, u, :, :], zero[:, :].unsqueeze(1).to_broadcast([P, DC, 2 * I]),
                                   ALU.add).then_inc(sm["gu_split_hi"], 1)
                pool.tensor_tensor(d_hi[:, u, :, :], d_raw[:, u, :, :], zero[0:IH, :].unsqueeze(1).to_broadcast([IH, 2, D]),
                                   ALU.add).then_inc(sm["gu_split_hi"], 1)
                wait(pool, "gu_split_hi", 2 * e + 2)
                pool.tensor_tensor(gu_lo[:, u, :, :], gu_raw[:, u, :, :], full(gu_hi[:, u, :, :]), ALU.subtract)\
                    .then_inc(sm["gu_split_lo"], 1)
                pool.tensor_tensor(d_lo[:, u, :, :], d_raw[:, u, :, :], full(d_hi[:, u, :, :]), ALU.subtract)\
                    .then_inc(sm["gu_ready"], 1)

            pool.wait_ge(sm["res_loaded"], 16)
            for t in range(TT):
                residual(t)
            def pair(i):
                split_expert(i, 0)
                split_expert(i, 1)

            experts(pool, pair)

        @block.tensor
        def _(pe):
            def product3(dst, lhs_hi, lhs_lo, rhs_hi, rhs_lo, first=True, last=True):
                nc.tensor.matmul(dst, lhs_hi, rhs_hi, start=first, stop=False)
                nc.tensor.matmul(dst, lhs_hi, rhs_lo, start=False, stop=False)
                return nc.tensor.matmul(dst, lhs_lo, rhs_hi, start=False, stop=last)

            def turn_tiles(src, group, sem_in, sem_out, evacuated):
                for c in range(DC):
                    n = DC * group + c
                    wait(pe, sem_in, TPC * group + TPC)
                    wait(pe, evacuated, n - 1)
                    for a in range(TPC):
                        last = nc.tensor.transpose(ps_t[:, n % 2, a * P:(a + 1) * P],
                                                   src[:, TPC * group + a, c * P:(c + 1) * P], ident[:, :])
                    last.then_inc(sm[sem_out], 1)

            pe.wait_ge(sm["ident_ready"], 1)
            for group in range(NCH):
                turn_tiles(xn_in, group, "xn_done", "xn_t", "xT_lo_done")
            pe.wait_ge(sm["xT_lo_done"], DC * NCH)

            def proj(dst, k, cols):
                for c in range(DC):
                    last = product3(dst, w_hi[k][:, c, :], w_lo[k][:, c, :], xT_hi[:, c, cols], xT_lo[:, c, cols],
                                    first=c == 0, last=c == DC - 1)
                return last

            def q_proj(h, j):
                m = NCH * h + j
                wait(pe, w_ready["q"], h + 1)
                free_side(h, j)
                proj(ps_a[:, (j + 1) % 2, :], "q", slice(j * CH, (j + 1) * CH)).then_inc(sm["q_ready"], 1)

            def free_side(h, j):
                m = NCH * h + j - 2
                wait(pe, "out_lo", m)
                wait(pe, "acc_done", 2 * m)
                if j == 1:
                    wait(pe, "v_full_done", TPC * h + 2)
                if j == 2:
                    wait(pe, "v_full_done", TPC * h + TPC)

            def k_proj(h):
                wait(pe, w_ready["k"], h + 1)
                for b in range(NCH):
                    wait(pe, "p_ready", NP * (TPC * NCH * h - 1) + PART_OF_BANK[b] + 1)
                    proj(ps_s[:, b * CH:(b + 1) * CH], "k", slice(b * CH, (b + 1) * CH)).then_inc(sm["k_ready"], 1)

            def v_proj(h, g, bank):
                wait(pe, w_ready["v"], h + 1)
                for a in range(TPC):
                    rows = slice((g * TPC + a) * P, (g * TPC + a + 1) * P)
                    for c in range(DC):
                        last = product3(ps_a[:, bank, a * DH:(a + 1) * DH], xT_hi[:, c, rows], xT_lo[:, c, rows],
                                        w_hi["v"][:, c, :], w_lo["v"][:, c, :], first=c == 0, last=c == DC - 1)
                last.then_inc(sm["v_ready"], 1)

            def scores(h, j, r, part):
                m = NCH * h + j
                if r == 0 and part == 0:
                    wait(pe, "q_lo", m + 1)
                for b in range(MAX_PARTS[part][0] // CH, MAX_PARTS[part][1] // CH):
                    if j == 0 and r == 0:
                        wait(pe, "k_lo", NCH * h + b + 1)
                    wait(pe, "p_ready", NP * (TPC * m + r - 1) + PART_OF_BANK[b] + 1)
                    cols = slice(b * CH, (b + 1) * CH)
                    last = product3(ps_s[:, cols], qT_hi[:, r * P:(r + 1) * P], qT_lo[:, r * P:(r + 1) * P],
                                    kT_hi[:, cols], kT_lo[:, cols])
                last.then_inc(sm["scores_ready"], 1)

            def turn_probs(h, j, k):
                n = KT * (NCH * h + j) + k
                if k == 0:
                    wait(pe, "p_ready", NP * TPC * (NCH * h + j + 1))
                wait(pe, "pt_lo", n - 1)
                for a in range(TPC):
                    last = nc.tensor.transpose(ps_t[:, k % 2, a * P:(a + 1) * P],
                                               probs[:, j % 2, a, k * P:(k + 1) * P], ident[:, :])
                last.then_inc(sm["t_ready"], 1)

            def weighted_values(h, j, k):
                n = KT * (NCH * h + j) + k
                if k == 0:
                    m = NCH * h + j
                    if has(h, j, 1):
                        wait(pe, "q_lo", m + 2)
                    wait(pe, "acc_done", 2 * (m - 1))
                    if j == 0:
                        wait(pe, "v_full_done", TPC * h + TPC - 1)
                    if j == 1:
                        wait(pe, "v_full_done", TPC * h + TPC)
                if j == 0 and k % TPC == 0:
                    wait(pe, "v_lo_done", TPC * h + k // TPC + 1)
                wait(pe, "pt_lo", n + 1)
                product3(ps_a[:, j % 2, :], v_hi[:, k, :], v_lo[:, k, :], pT_hi[:, k % RING, :], pT_lo[:, k % RING, :],
                         first=k == 0, last=k == KT - 1).then_inc(sm["pv_done"], 1)

            def out_proj(h, j, i):
                m = NCH * h + j - 1
                hp = h if j else h - 1
                wait(pe, "out_lo", m + 1)
                wait(pe, w_ready["o"], hp + 1)
                wait(pe, "acc_done", 2 * m + i)
                if i == 1 and j == NCH - 1 and has(h, j, 1):
                    wait(pe, "v_full_done", TPC * (h + 1) + 1)
                if i == 1 and j == 0 and has(h, j):
                    wait(pe, "v_full_done", TPC * h + TPC)
                for a in range(2):
                    rows = slice((2 * i + a) * P, (2 * i + a + 1) * P)
                    last = product3(ps_a[:, (j + 1) % 2, a * D:(a + 1) * D], oT_hi[:, rows], oT_lo[:, rows],
                                    w_hi["o"][:, :, :].rearrange("p c n -> p (c n)"),
                                    w_lo["o"][:, :, :].rearrange("p c n -> p (c n)"))
                last.then_inc(sm["oproj_ready"], 1)

            def body(h):
                for j in chunks_of(h):
                    nxt = (h, j + 1) if j < NCH - 1 else (h + 1, 0)
                    after = (h, j + 2) if j < NCH - 2 else (h + 1, j + 2 - NCH)
                    if isinstance(h, int) and h < 0:
                        q_proj(0, 0)
                    def key(k):
                        if k >= 2 and has(h, j):
                            weighted_values(h, j, k - 2)
                        if k < 2 and has(h, j, -1):
                            weighted_values(*((h, j - 1) if j else (h - 1, NCH - 1)), KT - 2 + k)
                        if has(h, j):
                            turn_probs(h, j, k)

                    for r in range(TPC):
                        new_head = j == NCH - 1 and r == 0 and has(h, j, 1)
                        if new_head:
                            k_proj(h + 1)
                            key(0)
                            key(1)
                        if has(h, j, 1):
                            scores(*nxt, r, 0)
                        if not new_head:
                            key(TPC * r + 0)
                        if has(h, j, 1):
                            scores(*nxt, r, 1)
                        if not new_head:
                            key(TPC * r + 1)
                        if has(h, j, 1):
                            scores(*nxt, r, 2)
                        if r == TPC - 1 and has(h, j, 2):
                            q_proj(*after)
                        if r in (1, 2) and has(h, j, -1):
                            out_proj(h, j, r - 1)
                        key(TPC * r + 2)
                        key(TPC * r + 3)
                        if j == NCH - 1 and r and has(h, j, 1):
                            g = r - 1
                            if has(h, j, -1):
                                wait(pe, "acc_done", 2 * (NCH * h + j - 1) + min(r, 2))
                            if r == TPC - 1 and has(h, j, 2):
                                wait(pe, "q_lo", NCH * h + j + 3)
                            if g:
                                wait(pe, "v_full_done", TPC * (h + 1) + g)
                            elif not has(h, j):
                                wait(pe, "q_lo", 1)
                            v_proj(h + 1, g, (j + 1) % 2)
                        if j == 0 and r == 1 and has(h, j):
                            wait(pe, "out_lo", NCH * h)
                            wait(pe, "acc_done", 2 * (NCH * h - 1) + 1)
                            wait(pe, "q_lo", NCH * h + 2)
                            v_proj(h, TPC - 1, (j + 1) % 2)

            heads(pe, body)

            for group in range(NCH):
                turn_tiles(xn2, group, "xn2_done", "xn2_t", "xT2_lo")
            pe.wait_ge(sm["xT2_lo"], DC * NCH)
            pe.wait_ge(sm["wr_lo_done"], 1)
            for t in range(TT):
                rows = slice(t * P, (t + 1) * P)
                for c in range(DC):
                    last = product3(ps_s[:, t * E:(t + 1) * E], xT_hi[:, c, rows], xT_lo[:, c, rows],
                                    wr_hi[:, c, :], wr_lo[:, c, :], first=c == 0, last=c == DC - 1)
            last.then_inc(sm["logits_ready"], 1)
            pe.wait_ge(sm["lsub_done"], 1)

            def gate_up(e, u, t):
                n = TT * e + t
                if t == 0:
                    wait(pe, "gu_ready", e + 1)
                wait(pe, "h_ready", n - 2)
                rows = slice(t * P, (t + 1) * P)
                b = t % 2
                for c in range(DC):
                    last = product3(ps_s[:, b * CH:b * CH + 2 * I], xT_hi[:, c, rows], xT_lo[:, c, rows],
                                    gu_hi[:, u, c, :], gu_lo[:, u, c, :], first=c == 0, last=c == DC - 1)
                last.then_inc(sm["h_gate"], 1)

            def turn_hidden(e, u, t):
                n = TT * e + t
                wait(pe, "h_ready", n + 1)
                wait(pe, "hT_lo_done", n - 1)
                for c in range(2):
                    last = nc.tensor.transpose(ps_t[0:IH, t % 2, c * P:(c + 1) * P],
                                               hid[:, t % 2, c * IH:(c + 1) * IH], ident[:, :])
                last.then_inc(sm["h_t"], 1)

            def down(e, u, t):
                n = TT * e + t
                wait(pe, "hT_lo_done", n + 1)
                wait(pe, "y_done", n - 1)
                for c in range(2):
                    last = product3(ps_a[:, t % 2, 0:D], hT_hi[:, t % 2, c, :], hT_lo[:, t % 2, c, :],
                                    d_hi[:, u, c, :], d_lo[:, u, c, :], first=c == 0, last=c == 1)
                last.then_inc(sm["down_ready"], 1)

            def pair(i):
                for u in range(2):
                    e = 2 * i + u
                    for t in range(TT + 2):
                        if t < TT:
                            gate_up(e, u, t)
                        if 1 <= t <= TT:
                            turn_hidden(e, u, t - 1)
                        if t >= 2:
                            down(e, u, t - 2)

            experts(pe, pair)

        @block.scalar
        def _(act):
            act.wait_ge(sm["eps_done"], 1)
            nc.scalar.activation(std[:, :], std[:, :], ACT.Sqrt).then_inc(sm["std_done"], 1)

            def turned(n, sem_in, sem_out):
                act.wait_ge(sm[sem_in], n + 1)
                group, c = n // DC, n % DC
                nc.scalar.activation(xT_hi[:, c, group * CH:(group + 1) * CH], ps_t[:, n % 2, :], ACT.Copy)\
                    .then_inc(sm[sem_out], 1)

            for n in range(DC * NCH):
                turned(n, "xn_t", "xT_hi_done")

            def exps(h, j, r, part):
                m = NCH * h + j
                wait(act, "shift_ready", TPC * m + r + 1)
                if r == 0 and part == 0:
                    wait(act, "t_ready", KT * (m - 1))
                cols = slice(*EXP_PARTS[part])
                nc.scalar.activation(probs[:, j % 2, r, cols], ps_s[:, cols], ACT.Exp, bias=shift[:, j % 2, r:r + 1],
                                     scale=SCALE, accum_out=sums[:, j % 2, r, part:part + 1])\
                    .then_inc(sm["p_ready"], 1)

            def probs_hi(h, j, k):
                n = KT * (NCH * h + j) + k
                wait(act, "t_ready", n + 1)
                wait(act, "pv_done", n - RING + 1)
                nc.scalar.activation(pT_hi[:, k % RING, :], ps_t[:, k % 2, :], ACT.Copy).then_inc(sm["pt_hi"], 1)

            def out_hi(h, j):
                m = NCH * h + j - 1
                wait(act, "pv_done", KT * (m + 1))
                wait(act, "oproj_ready", 2 * m)
                nc.scalar.activation(oT_hi[:, :], ps_a[:, (j + 1) % 2, :], ACT.Copy).then_inc(sm["out_hi"], 1)

            def q_hi(h, j):
                wait(act, "q_ready", NCH * h + j + 1)
                nc.scalar.activation(qT_hi[:, :], ps_a[:, (j + 1) % 2, :], ACT.Identity,
                                     bias=bias_now["q"][:, :]).then_inc(sm["q_hi"], 1)

            def k_hi(h, b):
                wait(act, "k_ready", NCH * h + b + 1)
                cols = slice(b * CH, (b + 1) * CH)
                nc.scalar.activation(kT_hi[:, cols], ps_s[:, cols], ACT.Identity,
                                     bias=bias_now["k"][:, :]).then_inc(sm["k_hi"], 1)

            def body(h):
                for j in chunks_of(h):
                    nxt = (h, j + 1) if j < NCH - 1 else (h + 1, 0)
                    after = (h, j + 2) if j < NCH - 2 else (h + 1, j + 2 - NCH)
                    if isinstance(h, int) and h < 0:
                        q_hi(0, 0)
                    for r in range(TPC):
                        new_head = j == NCH - 1 and r == 0 and has(h, j, 1)
                        k = TPC * r
                        if new_head:
                            for b in range(NCH):
                                k_hi(h + 1, b)
                            if has(h, j):
                                probs_hi(h, j, 0)
                                probs_hi(h, j, 1)
                        if has(h, j) and not new_head:
                            probs_hi(h, j, k + 0)
                        if has(h, j) and not new_head:
                            probs_hi(h, j, k + 1)
                        if r == 0 and has(h, j, -1):
                            out_hi(h, j)
                        if has(h, j, 1):
                            exps(*nxt, r, 0)
                        if r == TPC - 1 and has(h, j, 2):
                            q_hi(*after)
                        if has(h, j):
                            probs_hi(h, j, k + 2)
                        if has(h, j, 1):
                            exps(*nxt, r, 1)
                        if has(h, j):
                            probs_hi(h, j, k + 3)
                        if has(h, j, 1):
                            exps(*nxt, r, 2)

            heads(act, body)

            for s_in, s_out in (("eps1", "std1"), ("eps2", "std2")):
                act.wait_ge(sm[s_in], 1)
                nc.scalar.activation(std[:, :], std[:, :], ACT.Sqrt).then_inc(sm[s_out], 1)
            for n in range(DC * NCH):
                turned(n, "xn2_t", "xT2_hi")
            act.wait_ge(sm["lsub_done"], 1)
            nc.scalar.activation(ex[:, :, :], ex[:, :, :], ACT.Exp).then_inc(sm["ex_done"], 1)

            def gates(e, t):
                n = TT * e + t
                wait(act, "h_gate", n + 1)
                wait(act, "h_ready", n - 1)
                nc.scalar.activation(gate[:, t % 2, :], ps_s[:, (t % 2) * CH:(t % 2) * CH + I], ACT.Silu)\
                    .then_inc(sm["gu_gate"], 1)

            def hidden_hi(e, t):
                n = TT * e + t
                wait(act, "h_t", n + 1)
                wait(act, "down_ready", n - 1)
                nc.scalar.activation(hT_hi[:, t % 2, :, :],
                                     ps_t[0:IH, t % 2, 0:2 * P].rearrange("p (c n) -> p c n", c=2), ACT.Copy)\
                    .then_inc(sm["hT_hi_done"], 1)

            def pair(i):
                for u in range(2):
                    e = 2 * i + u
                    for t in range(TT + 1):
                        if t < TT:
                            gates(e, t)
                        if t >= 1:
                            hidden_hi(e, t - 1)
            experts(act, pair)
            act.wait_ge(sm["eps3"], 1)
            nc.scalar.activation(std[:, :], std[:, :], ACT.Sqrt).then_inc(sm["std3"], 1)

        @block.vector
        def _(dve):
            V = nc.vector

            def moments(src, t, s_stat, s_aggr, ready=None):
                if ready is not None:
                    dve.wait_ge(sm[ready[0]], ready[1])
                V.bn_stats(stats[:, t, :], src[:, t, :]).then_inc(sm[s_stat], 1)
                dve.wait_ge(sm[s_stat], t + 1)
                V.bn_aggr(mv[:, t, :], stats[:, t, :]).then_inc(sm[s_aggr], 1)

            def inverse_std(s_aggr, s_eps, s_std, s_rstd):
                dve.wait_ge(sm[s_aggr], TT)
                V.tensor_scalar(std[:, :], mv[:, :, 1], EPS, None, ALU.add).then_inc(sm[s_eps], 1)
                dve.wait_ge(sm[s_std], 1)
                V.reciprocal(rstd[:, :], std[:, :]).then_inc(sm[s_rstd], 1)
                dve.wait_ge(sm[s_rstd], 1)

            def normed(dst, src, t):
                return V.tensor_scalar(dst[:, t, :], src[:, t, :], mv[:, t, 0:1], rstd[:, t:t + 1],
                                       ALU.subtract, ALU.mult)

            def turned_lo(n, sem_in, sem_out):
                dve.wait_ge(sm[sem_in], n + 1)
                group, c = n // DC, n % DC
                cols = slice(group * CH, (group + 1) * CH)
                V.tensor_tensor(xT_lo[:, c, cols], ps_t[:, n % 2, :], full(xT_hi[:, c, cols]), ALU.subtract)\
                    .then_inc(sm[sem_out], 1)

            for t in range(TT):
                if t % TPC == 0:
                    dve.wait_ge(x_loaded[t // TPC], 16)
                moments(x_in, t, "stat_done", "aggr_done")
            inverse_std("aggr_done", "eps_done", "std_done", "rstd_done")
            for t in range(TT):
                normed(xn_in, x_in, t).then_inc(sm["xn_done"], 1)
            for n in range(DC * NCH):
                turned_lo(n, "xT_hi_done", "xT_lo_done")
            dve.wait_ge(sm["bo_loaded"], 16)
            dve.wait_ge(sm["bias_loaded"], 48)

            def part_of_max(h, j, r, part):
                n = NP * (TPC * (NCH * h + j) + r) + part
                wait(dve, "scores_ready", n + 1)
                V.tensor_reduce(part_max[:, j % 2, r, part:part + 1], ps_s[:, slice(*MAX_PARTS[part])], AX.X, ALU.max)\
                    .then_inc(sm["max_part"], 1)

            def first_max(h, j, r):
                wait(dve, "max_part", NP * (TPC * (NCH * h + j) + r) + 2)
                V.tensor_tensor(part_max[:, j % 2, r, NP:NP + 1], part_max[:, j % 2, r, 0:1],
                                part_max[:, j % 2, r, 1:2], ALU.max).then_inc(sm["max_first"], 1)

            def row_shift(h, j, r):
                n = TPC * (NCH * h + j) + r
                wait(dve, "max_first", n + 1)
                wait(dve, "max_part", NP * (n + 1))
                V.tensor_scalar(shift[:, j % 2, r:r + 1], part_max[:, j % 2, r, 2:3], part_max[:, j % 2, r, NP:NP + 1],
                                -SCALE, ALU.max, ALU.mult).then_inc(sm["shift_ready"], 1)

            def probs_lo(h, j, k):
                n = KT * (NCH * h + j) + k
                wait(dve, "pt_hi", n + 1)
                V.tensor_tensor(pT_lo[:, k % RING, :], ps_t[:, k % 2, :], full(pT_hi[:, k % RING, :]), ALU.subtract)\
                    .then_inc(sm["pt_lo"], 1)

            def out_lo(h, j):
                wait(dve, "out_hi", NCH * h + j)
                V.tensor_tensor(oT_lo[:, :], ps_a[:, (j + 1) % 2, :], full(oT_hi[:, :]), ALU.subtract)\
                    .then_inc(sm["out_lo"], 1)

            def row_sums(h, j):
                m = NCH * h + j
                wait(dve, "p_ready", NP * TPC * (m + 1))
                V.tensor_reduce(total[:, j % 2, :], sums[:, j % 2, :, :], AX.X, ALU.add)\
                    .then_inc(sm["total_done"], 1)
                wait(dve, "total_done", m + 1)
                V.reciprocal(rinv[:, j % 2, :], total[:, j % 2, :]).then_inc(sm["rinv_ready"], 1)

            def add_out(h, j, i):
                m = NCH * h + j - 1
                jp = (j - 1) % NCH
                wait(dve, "oproj_ready", 2 * m + i + 1)
                if i == 0:
                    wait(dve, "rinv_ready", m + 1)
                for a in range(2):
                    t = jp * TPC + 2 * i + a
                    ins = V.scalar_tensor_tensor(acc[:, t, :], ps_a[:, (j + 1) % 2, a * D:(a + 1) * D],
                                                 rinv[:, jp % 2, 2 * i + a:2 * i + a + 1], acc[:, t, :],
                                                 ALU.mult, ALU.add)
                ins.then_inc(sm["acc_done"], 1)

            def q_lo(h, j):
                wait(dve, "q_hi", NCH * h + j + 1)
                V.scalar_tensor_tensor(qT_lo[:, :], ps_a[:, (j + 1) % 2, :], bias_now["q"][:, :], full(qT_hi[:, :]),
                                       ALU.add, ALU.subtract).then_inc(sm["q_lo"], 1)

            def k_lo(h, b):
                wait(dve, "k_hi", NCH * h + b + 1)
                cols = slice(b * CH, (b + 1) * CH)
                V.scalar_tensor_tensor(kT_lo[:, cols], ps_s[:, cols], bias_now["k"][:, :], full(kT_hi[:, cols]),
                                       ALU.add, ALU.subtract).then_inc(sm["k_lo"], 1)

            def values(h, g, bank):
                n = TPC * h + g
                wait(dve, "v_ready", n + 1)
                wait(dve, "v_lo_done", n)
                src = ps_a[:, bank, :].rearrange("p (a d) -> p a d", d=DH)
                bias = bias_v[:, bass.ds(h * DH, DH)].unsqueeze(1).to_broadcast([P, TPC, DH])
                V.tensor_tensor(v_hi[:, g * TPC:(g + 1) * TPC, :], src, bias, ALU.add)
                V.tensor_tensor(v_full[:, :, :], src, bias, ALU.add).then_inc(sm["v_full_done"], 1)

            def body(h):
                for j in chunks_of(h):
                    nxt = (h, j + 1) if j < NCH - 1 else (h + 1, 0)
                    after = (h, j + 2) if j < NCH - 2 else (h + 1, j + 2 - NCH)
                    if isinstance(h, int) and h < 0:
                        q_lo(0, 0)
                    for r in range(TPC):
                        new_head = j == NCH - 1 and r == 0 and has(h, j, 1)
                        k = TPC * r
                        if new_head:
                            for b in range(NCH):
                                k_lo(h + 1, b)
                            if has(h, j):
                                probs_lo(h, j, 0)
                                probs_lo(h, j, 1)
                        if has(h, j, 1):
                            part_of_max(*nxt, r, 0)
                        if has(h, j) and not new_head:
                            probs_lo(h, j, k + 0)
                        if has(h, j, 1):
                            part_of_max(*nxt, r, 1)
                        if has(h, j, 1):
                            first_max(*nxt, r)
                        if has(h, j, 1):
                            part_of_max(*nxt, r, 2)
                        if has(h, j, 1):
                            row_shift(*nxt, r)
                        if has(h, j) and not new_head:
                            probs_lo(h, j, k + 1)
                        if r == 0 and has(h, j, -1):
                            out_lo(h, j)
                        if r in (1, 2) and has(h, j, -1):
                            add_out(h, j, r - 1)
                        if r == TPC - 1 and has(h, j, 2):
                            q_lo(*after)
                        if has(h, j):
                            probs_lo(h, j, k + 2)
                        if has(h, j):
                            probs_lo(h, j, k + 3)
                        if r == 0 and has(h, j):
                            row_sums(h, j)
                        if r == TPC - 1 and isinstance(h, int) and (h, j) > (H - 1, 0):
                            wait(dve, "acc_done", 2 * (NCH * h + j))
                            for t in range((NCH * h + j - 1) % NCH * TPC, ((NCH * h + j - 1) % NCH + 1) * TPC):
                                moments(acc, t, "stat1", "aggr1")
                        if j == NCH - 1 and r and has(h, j, 1):
                            values(h + 1, r - 1, (j + 1) % 2)
                        if j == 0 and r == 1 and has(h, j):
                            values(h, TPC - 1, (j + 1) % 2)

            heads(dve, body)

            dve.wait_ge(sm["acc_done"], 2 * CHUNKS)
            inverse_std("aggr1", "eps1", "std1", "rstd1")
            for t in range(TT):
                normed(acc, acc, t).then_inc(sm["z_norm"], 1)
            for t in range(TT):
                moments(x1, t, "stat2", "aggr2", ("x1_done", t + 1))
            inverse_std("aggr2", "eps2", "std2", "rstd2")
            for t in range(TT):
                normed(xn2, x1, t).then_inc(sm["xn2_done"], 1)
            for n in range(DC * NCH):
                turned_lo(n, "xT2_hi", "xT2_lo")

            dve.wait_ge(sm["logits_ready"], 1)
            logits = ps_s[:, 0:TT * E].rearrange("p (t e) -> p t e", e=E)
            V.tensor_reduce(lmax[:, :], logits, AX.X, ALU.max).then_inc(sm["lmax_done"], 1)
            dve.wait_ge(sm["lmax_done"], 1)
            V.tensor_tensor(ex[:, :, :], logits, lmax[:, :].unsqueeze(2).to_broadcast([P, TT, E]), ALU.subtract)\
                .then_inc(sm["lsub_done"], 1)
            dve.wait_ge(sm["ex_done"], 1)
            steps = 0
            for a in range(E):
                for lo, hi, op in ((0, a + 1, ALU.is_gt), (a + 1, E, ALU.is_ge)):
                    if lo < hi:
                        V.tensor_tensor(cmp[:, a, :, lo:hi], ex[:, :, a:a + 1].to_broadcast([P, TT, hi - lo]),
                                        ex[:, :, lo:hi], op).then_inc(sm["rank_step"], 1)
                        steps += 1
            half = E // 2
            while half:
                dve.wait_ge(sm["rank_step"], steps)
                V.tensor_tensor(cmp[:, 0:half, :, :], cmp[:, 0:half, :, :], cmp[:, half:2 * half, :, :], ALU.add)\
                    .then_inc(sm["rank_step"], 1)
                steps += 1
                half //= 2
            dve.wait_ge(sm["rank_step"], steps)
            V.scalar_tensor_tensor(comb[:, :, :], cmp[:, 0, :, :], 1.5, ex[:, :, :], ALU.is_lt, ALU.mult)\
                .then_inc(sm["sel_done"], 1)
            dve.wait_ge(sm["sel_done"], 1)
            V.tensor_reduce(wsum[:, :], comb[:, :, :], AX.X, ALU.add).then_inc(sm["comb_step"], 1)
            dve.wait_ge(sm["comb_step"], 1)
            V.reciprocal(wsum[:, :], wsum[:, :]).then_inc(sm["comb_step"], 1)
            dve.wait_ge(sm["comb_step"], 2)
            V.tensor_tensor(comb[:, :, :], comb[:, :, :], wsum[:, :].unsqueeze(2).to_broadcast([P, TT, E]), ALU.mult)\
                .then_inc(sm["comb_ready"], 1)
            dve.wait_ge(sm["comb_ready"], 1)
            dve.wait_ge(sm["y_zero"], 1)

            def hidden(e, t):
                n = TT * e + t
                wait(dve, "gu_gate", n + 1)
                wait(dve, "h_t", n - 1)
                V.scalar_tensor_tensor(hid[:, t % 2, :], gate[:, t % 2, :], comb[:, t, bass.ds(e, 1)],
                                       ps_s[:, (t % 2) * CH + I:(t % 2) * CH + 2 * I], ALU.mult, ALU.mult)\
                    .then_inc(sm["h_ready"], 1)

            def hidden_lo(e, t):
                n = TT * e + t
                wait(dve, "hT_hi_done", n + 1)
                V.tensor_tensor(hT_lo[:, t % 2, :, :], ps_t[0:IH, t % 2, 0:2 * P].rearrange("p (c n) -> p c n", c=2),
                                full(hT_hi[:, t % 2, :, :]), ALU.subtract).then_inc(sm["hT_lo_done"], 1)

            def add_expert(e, t):
                wait(dve, "down_ready", TT * e + t + 1)
                V.tensor_tensor(y[:, t, :], ps_a[:, t % 2, 0:D], y[:, t, :], ALU.add).then_inc(sm["y_done"], 1)

            def pair(i):
                for u in range(2):
                    e = 2 * i + u
                    for t in range(TT + 2):
                        if t < TT:
                            hidden(e, t)
                        if 1 <= t <= TT:
                            hidden_lo(e, t - 1)
                        if t >= 2:
                            add_expert(e, t - 2)

            experts(dve, pair)

            dve.wait_ge(sm["y_done"], TT * E)
            for t in range(TT):
                moments(y, t, "stat3", "aggr3")
            inverse_std("aggr3", "eps3", "std3", "rstd3")
            for t in range(TT):
                normed(y, y, t).then_inc(sm["yn_done"], 1)
                dve.wait_ge(sm["yn_done"], t + 1)
                V.tensor_tensor(xn2[:, t, :], x1[:, t, :], y[:, t, :], ALU.add).then_inc(sm["out_ready"], 1)


_INS = ["x", "wq_codes", "wq_scales", "bq", "wk_codes", "wk_scales", "bk", "wv_codes", "wv_scales", "bv",
        "wo_codes", "wo_scales", "bo"]
_FFN = ["Wr", "Wg", "Wu", "Wd"]


def kernel(**inputs):
    import numpy as np
    import concourse.bacc as bacc
    from concourse import mybir
    from concourse.bass_utils import run_bass_kernel_spmd

    nc = bacc.Bacc("TRN2", target_bir_lowering=False, num_devices=1)
    arrays, aps = {}, []
    for name in [f"L0_attn_{n}" for n in _INS] + [f"L0_ffn_{n}" for n in _FFN]:
        a = np.ascontiguousarray(inputs[name])
        arrays[f"in_{name}"] = a
        aps.append(nc.dram_tensor(f"in_{name}", a.shape, mybir.dt.from_np(a.dtype), kind="ExternalInput").ap())
    shape = inputs["L0_attn_x"].shape
    aps.append(nc.dram_tensor("layer_out", shape, mybir.dt.float32, kind="ExternalOutput").ap())
    sandwich_layer(nc, *aps)
    r = run_bass_kernel_spmd(nc, [arrays], core_ids=[0])
    return r.results[0]["layer_out"]
```
